# Optimizing a Trainium2 kernel written in Bass

```python
import numpy as np
import jax
import jax.numpy as jnp

def _softmax(x, axis=-1):
    return jax.nn.softmax(x, axis=axis)

def _gelu(x):
    return jax.nn.gelu(x, approximate=True)

def _silu(x):
    return jax.nn.silu(x)

def _sigmoid(x):
    return jax.nn.sigmoid(x)

def _layernorm(x, axis=-1, eps=1e-05):
    m = jnp.mean(x, axis=axis, keepdims=True)
    v = jnp.var(x, axis=axis, keepdims=True)
    return (x - m) / jnp.sqrt(v + eps)

def _scatter_add(tgt, idx, src, axis=0):
    return tgt.at[idx].add(src)

def _segment_sum(src, seg, n):
    return jax.ops.segment_sum(src, seg, n)
kernel_name = 'mk_early_fusion_d1_tok_img768_r4_32d4cd'

def setup_inputs(seed: int=0):
    np.random.seed(seed)
    _w = jnp.asarray

    def _rec_inputs():
        import jax
        import jax.numpy as jnp
        _rk = jax.random.key(seed)
        x = -0.000596345 + 1.00056 * jax.random.normal(jax.random.fold_in(_rk, 1), (8, 3, 64, 64), jnp.float32)
        txt = -0.000190561 + 0.886117 * jax.random.normal(jax.random.fold_in(_rk, 2), (8, 128, 192), jnp.float32)
        return (x, txt)
    x, txt = _rec_inputs()

    def _L0_tok_setup():
        import jax, jax.numpy as jnp
        import numpy as np
        B = 16
        IMG = 64
        CH = 3
        EMBED = 64
        GP = 16
        PRE = [1, 2, 4]
        N_LEVELS = 3
        FUSED = EMBED * N_LEVELS

        def hilbert_flat_indices(n):
            t = np.arange(n * n, dtype=np.int64)
            x = np.zeros(n * n, dtype=np.int64)
            y = np.zeros(n * n, dtype=np.int64)
            s = 1
            while s < n:
                rx = 1 & t // 2
                ry = 1 & (t ^ rx)
                swap = ry == 0
                flip = swap & (rx == 1)
                x = np.where(flip, s - 1 - x, x)
                y = np.where(flip, s - 1 - y, y)
                x2 = np.where(swap, y, x)
                y2 = np.where(swap, x, y)
                x, y = (x2, y2)
                x = x + s * rx
                y = y + s * ry
                t = t // 4
                s *= 2
            return y * n + x

        def _level(x, idx, W, b, p, gp):
            Bsz, C, H, _ = x.shape
            h = H // p
            t = x.reshape(Bsz, C, h, p, h, p).transpose(0, 2, 4, 3, 5, 1).reshape(Bsz, h * h, p * p * C)
            t = t[:, idx]
            t = t.reshape(Bsz, h * h // gp, gp * p * p * C)
            return t @ W.T + b

        def _interp_linear(x, n_out):
            L = x.shape[1]
            pos = (jnp.arange(n_out, dtype=jnp.float32) + 0.5) * (L / n_out) - 0.5
            pos = jnp.clip(pos, 0.0, L - 1)
            i0 = jnp.floor(pos).astype(jnp.int32)
            i1 = jnp.minimum(i0 + 1, L - 1)
            w = (pos - i0).astype(x.dtype)
            return x[:, i0] * (1.0 - w)[None, :, None] + x[:, i1] * w[None, :, None]
        key = jax.random.key(seed)
        ks = jax.random.split(key, 9)
        inp = {'x': jax.random.normal(ks[0], (B, CH, IMG, IMG), jnp.float32)}
        for i, p in enumerate(PRE):
            din = CH * p * p * GP
            inp[f'W{i}'] = jax.random.normal(ks[1 + 2 * i], (EMBED, din), jnp.float32) * din ** (-0.5)
            inp[f'b{i}'] = jax.random.normal(ks[2 + 2 * i], (EMBED,), jnp.float32) * 0.02
        inp['Wf'] = jax.random.normal(ks[7], (FUSED, FUSED), jnp.float32) * FUSED ** (-0.5)
        inp['bf'] = jax.random.normal(ks[8], (FUSED,), jnp.float32) * 0.02
        for i, p in enumerate(PRE):
            inp[f'idx{i}'] = jnp.asarray(hilbert_flat_indices(IMG // p), jnp.int32)
        return inp
    _L0_tok_all = _L0_tok_setup()
    _L0_tok_in = {k: v for k, v in _L0_tok_all.items() if k in ('W0', 'b0', 'W1', 'b1', 'W2', 'b2', 'Wf', 'bf', 'idx0', 'idx1', 'idx2')}
    del _L0_tok_all

    def _L0_attn_setup():
        import jax, jax.numpy as jnp
        import numpy as np
        INIT_STD = 0.05
        key = jax.random.key(seed)
        k1, k2, k3 = jax.random.split(key, 3)
        b, p, d = (2, 512, 192)
        h, n = (12, 64)
        x = jax.random.normal(k1, (b, p, d), dtype=jnp.float32)
        w_qkv = INIT_STD * jax.random.normal(k2, (h, 3, d, n), dtype=jnp.float32)
        w_o = INIT_STD * jax.random.normal(k3, (h * n, d), dtype=jnp.float32)
        return {'x': x, 'w_qkv': w_qkv, 'w_o': w_o}
    _L0_attn_all = _L0_attn_setup()
    _L0_attn_in = {k: v for k, v in _L0_attn_all.items() if k in ('w_qkv', 'w_o')}
    del _L0_attn_all

    def _L0_ffn_setup():
        import jax, jax.numpy as jnp
        import numpy as np
        B, S, H, F, E, TOP_K = (4, 512, 192, 768, 8, 2)
        key = jax.random.key(seed)
        ks = jax.random.split(key, 6)
        x = jax.random.normal(ks[0], (B, S, H), dtype=jnp.float32)
        Wr = jax.random.normal(ks[1], (E, H), dtype=jnp.float32) * 0.02
        Wi = jax.random.normal(ks[2], (E, F, H), dtype=jnp.float32) * 0.02
        bi = jnp.zeros((E, F), dtype=jnp.float32)
        Wo = jax.random.normal(ks[3], (E, H, F), dtype=jnp.float32) * 0.02
        bo = jnp.zeros((E, H), dtype=jnp.float32)
        return {'x': x, 'Wr': Wr, 'Wi': Wi, 'bi': bi, 'Wo': Wo, 'bo': bo}
    _L0_ffn_all = _L0_ffn_setup()
    _L0_ffn_in = {k: v for k, v in _L0_ffn_all.items() if k in ('Wr', 'Wi', 'bi', 'Wo', 'bo')}
    del _L0_ffn_all
    return {'x': x, 'txt': txt, 'L0_tok_W0': _L0_tok_in['W0'], 'L0_tok_b0': _L0_tok_in['b0'], 'L0_tok_W1': _L0_tok_in['W1'], 'L0_tok_b1': _L0_tok_in['b1'], 'L0_tok_W2': _L0_tok_in['W2'], 'L0_tok_b2': _L0_tok_in['b2'], 'L0_tok_Wf': _L0_tok_in['Wf'], 'L0_tok_bf': _L0_tok_in['bf'], 'L0_tok_idx0': _L0_tok_in['idx0'], 'L0_tok_idx1': _L0_tok_in['idx1'], 'L0_tok_idx2': _L0_tok_in['idx2'], 'L0_attn_w_qkv': _L0_attn_in['w_qkv'], 'L0_attn_w_o': _L0_attn_in['w_o'], 'L0_ffn_Wr': _L0_ffn_in['Wr'], 'L0_ffn_Wi': _L0_ffn_in['Wi'], 'L0_ffn_bi': _L0_ffn_in['bi'], 'L0_ffn_Wo': _L0_ffn_in['Wo'], 'L0_ffn_bo': _L0_ffn_in['bo']}

def reference(x, txt, L0_tok_W0, L0_tok_b0, L0_tok_W1, L0_tok_b1, L0_tok_W2, L0_tok_b2, L0_tok_Wf, L0_tok_bf, L0_tok_idx0, L0_tok_idx1, L0_tok_idx2, L0_attn_w_qkv, L0_attn_w_o, L0_ffn_Wr, L0_ffn_Wi, L0_ffn_bi, L0_ffn_Wo, L0_ffn_bo):
    import jax
    import jax.numpy as jnp

    def _L0_tok_ref(x, W0, b0, W1, b1, W2, b2, Wf, bf, idx0, idx1, idx2):
        import jax, jax.numpy as jnp
        import numpy as np
        B = 16
        IMG = 64
        CH = 3
        EMBED = 64
        GP = 16
        PRE = [1, 2, 4]
        N_LEVELS = 3
        FUSED = EMBED * N_LEVELS

        def hilbert_flat_indices(n):
            t = np.arange(n * n, dtype=np.int64)
            x = np.zeros(n * n, dtype=np.int64)
            y = np.zeros(n * n, dtype=np.int64)
            s = 1
            while s < n:
                rx = 1 & t // 2
                ry = 1 & (t ^ rx)
                swap = ry == 0
                flip = swap & (rx == 1)
                x = np.where(flip, s - 1 - x, x)
                y = np.where(flip, s - 1 - y, y)
                x2 = np.where(swap, y, x)
                y2 = np.where(swap, x, y)
                x, y = (x2, y2)
                x = x + s * rx
                y = y + s * ry
                t = t // 4
                s *= 2
            return y * n + x

        def _level(x, idx, W, b, p, gp):
            Bsz, C, H, _ = x.shape
            h = H // p
            t = x.reshape(Bsz, C, h, p, h, p).transpose(0, 2, 4, 3, 5, 1).reshape(Bsz, h * h, p * p * C)
            t = t[:, idx]
            t = t.reshape(Bsz, h * h // gp, gp * p * p * C)
            return t @ W.T + b

        def _interp_linear(x, n_out):
            L = x.shape[1]
            pos = (jnp.arange(n_out, dtype=jnp.float32) + 0.5) * (L / n_out) - 0.5
            pos = jnp.clip(pos, 0.0, L - 1)
            i0 = jnp.floor(pos).astype(jnp.int32)
            i1 = jnp.minimum(i0 + 1, L - 1)
            w = (pos - i0).astype(x.dtype)
            return x[:, i0] * (1.0 - w)[None, :, None] + x[:, i1] * w[None, :, None]
        Ws = [(idx0, W0, b0, PRE[0]), (idx1, W1, b1, PRE[1]), (idx2, W2, b2, PRE[2])]
        outs = [_level(x, idx, W, b, p, GP) for idx, W, b, p in Ws]
        n_tokens = outs[0].shape[1]
        outs = [outs[0]] + [_interp_linear(o, n_tokens) for o in outs[1:]]
        y = jnp.concatenate(outs, axis=-1)
        return y @ Wf.T + bf

    def _L0_attn_ref(x, w_qkv, w_o):
        import jax, jax.numpy as jnp
        import numpy as np
        INIT_STD = 0.05
        head_dim = w_qkv.shape[-1]
        qkv = jnp.einsum('bpv,havn->bhapn', x, w_qkv)
        q, k, v = (qkv[:, :, 0], qkv[:, :, 1], qkv[:, :, 2])
        scale = jnp.sqrt(jnp.asarray(head_dim, dtype=x.dtype))
        scores = jnp.einsum('bhqn,bhkn->bhqk', q, k) / scale
        attn = jax.nn.softmax(scores, axis=-1)
        out = jnp.einsum('bhqk,bhkn->bhqn', attn, v)
        b, h, p, n = out.shape
        out = out.transpose(0, 2, 1, 3).reshape(b, p, h * n)
        return jnp.einsum('bpi,ij->bpj', out, w_o)

    def _L0_ffn_ref(x, Wr, Wi, bi, Wo, bo):
        import jax, jax.numpy as jnp
        import numpy as np
        B, S, H, F, E, TOP_K = (4, 512, 192, 768, 8, 2)
        xf = x.reshape(-1, x.shape[-1])
        router_logits = jnp.einsum('th,eh->te', xf, Wr)
        topk_vals, topk_idx = jax.lax.top_k(router_logits, TOP_K)
        routing_weights = jax.nn.softmax(topk_vals, axis=-1)
        h = jnp.einsum('th,efh->etf', xf, Wi) + bi[:, None, :]
        h = jax.nn.gelu(h, approximate=False)
        expert_out = jnp.einsum('etf,ehf->eth', h, Wo) + bo[:, None, :]
        expert_out = jnp.transpose(expert_out, (1, 0, 2))
        gathered = jnp.take_along_axis(expert_out, topk_idx[:, :, None], axis=1)
        out = jnp.einsum('tk,tkh->th', routing_weights, gathered)
        return out.reshape(x.shape)
    h = _L0_tok_ref(x, L0_tok_W0, L0_tok_b0, L0_tok_W1, L0_tok_b1, L0_tok_W2, L0_tok_b2, L0_tok_Wf, L0_tok_bf, L0_tok_idx0, L0_tok_idx1, L0_tok_idx2)
    h = jnp.concatenate([h, txt], axis=1)
    h = h + _L0_attn_ref(_layernorm(h, axis=-1), L0_attn_w_qkv, L0_attn_w_o)
    h = h + _L0_ffn_ref(_layernorm(h, axis=-1), L0_ffn_Wr, L0_ffn_Wi, L0_ffn_bi, L0_ffn_Wo, L0_ffn_bo)
    return h

_drawn_inputs = setup_inputs


def setup_inputs(seed=0):
    import zlib

    import numpy as np

    out = dict(_drawn_inputs(seed))
    spreads = {'L0_ffn_bi': (0.0, 0.354), 'L0_ffn_bo': (0.0, 0.1)}
    factors = {'L0_tok_b0': 3.407, 'L0_tok_b1': 3.117, 'L0_tok_b2': 3.042}
    for name, (base, spread) in spreads.items():
        noise = np.random.default_rng([zlib.crc32(name.encode()), seed]).standard_normal(out[name].shape)
        drawn = base * np.exp(spread * noise) if base else spread * noise
        out[name] = jnp.asarray(drawn.astype(out[name].dtype))
    for name, factor in factors.items():
        out[name] = (out[name] * factor).astype(out[name].dtype)
    return out
```

```python
from contextlib import ExitStack

import numpy as np
import concourse.bass as bass
from concourse import mybir

F32 = mybir.dt.float32
I32 = mybir.dt.int32
U32 = mybir.dt.uint32
ALU = mybir.AluOpType
ACT = mybir.ActivationFunctionType
AX_X = mybir.AxisListType.X

P = 128
B = 8
IMG, CH, GP = 64, 3, 16
TOK_IMG = IMG * IMG // GP
TOK_TXT = 128
SEQ = TOK_IMG + TOK_TXT
D = 192
KH = D // 2
MT = SEQ // P
NT = B * MT
NTOK = NT * P
HEADS, DH = 12, 64
NPAIR = HEADS // 2
DI = HEADS * DH
EMB = 64
E = 8
F = 768
FT = F // P
FH = F // 2
NBLK = 2 * NT + E
NBLK_LOADED = NBLK + 4
ROW = D + 2
EPS = 1e-5
PRIMED = 1


def fused_layer_kernel(nc, xp0, xp1, xp2, txt, W0T, b0, W1T, b1, W2T, b2, WfT, bf, idx0, idx1, idx2,
                       wqkv, wo, WrT, WiT, bi, WoT, bo, base2, ident_c, tri_c, A1, A2, expert_of, keep,
                       block_no, dest_c, xg_init, xg, z, out):
    ctx = ExitStack()

    def sb(stack, name, shape, dt=F32):
        return stack.enter_context(nc.sbuf_tensor(name, shape, dt))

    def sem(name):
        return ctx.enter_context(nc.semaphore(name))

    with ctx:
        h = sb(ctx, "h", [P, NT, D])
        wi = sb(ctx, "wi", [KH + 1, 2, E * F])
        wo2 = sb(ctx, "wo2", [P, E * FT, D])
        bo_bc = sb(ctx, "bo_bc", [P, E * D])
        ident = sb(ctx, "ident", [P, P])
        tri = sb(ctx, "tri", [P, P])
        ones = sb(ctx, "ones", [P, P])
        wr = sb(ctx, "wr", [KH, 2, E])
        epsc = sb(ctx, "epsc", [P, 1])
        stats = sb(ctx, "stats", [P, NT, 6])
        mv = sb(ctx, "mv", [P, NT, 2])
        rstd = sb(ctx, "rstd", [P, NT])

        tk = ExitStack()
        i0 = sb(tk, "i0", [P, 2, GP], I32)
        i1 = sb(tk, "i1", [64, GP], I32)
        i2 = sb(tk, "i2", [P, GP], I32)
        i2b = sb(tk, "i2b", [P, GP], I32)
        g0 = sb(tk, "g0", [P, 2, GP, B * 3])
        g1 = sb(tk, "g1", [64, GP, B * 12])
        g2 = sb(tk, "g2", [P, GP, 48])
        g0b = sb(tk, "g0b", [P, 2, B, GP * 3])
        g1b = sb(tk, "g1b", [64, B, GP * 12])
        g0t = sb(tk, "g0t", [48, B * TOK_IMG])
        g1t = sb(tk, "g1t", [96, 2, 512])
        g2t = sb(tk, "g2t", [96, 8, P])
        e1 = sb(tk, "e1", [64, 512])
        e2 = sb(tk, "e2", [P, EMB])
        ya = sb(tk, "ya", [P, B * TOK_IMG])
        yb = sb(tk, "yb", [EMB, B * TOK_IMG])
        a1 = sb(tk, "a1", [64, TOK_IMG])
        a2 = sb(tk, "a2", [P, B, TOK_IMG])
        w0 = sb(tk, "w0", [48, EMB])
        w1 = sb(tk, "w1", [96, 2, EMB])
        w2 = sb(tk, "w2", [96, 8, EMB])
        wfa = sb(tk, "wfa", [P, D])
        wfb = sb(tk, "wfb", [EMB, D])
        bca = sb(tk, "bca", [P, 1])
        bcb = sb(tk, "bcb", [EMB, 1])
        bf_bc = sb(tk, "bf_bc", [P, D])
        tk.close()

        at = ExitStack()
        wq = sb(at, "wq", [KH, 2, 3 * DI])
        wot = sb(at, "wot", [P, NPAIR, D])
        xnb = sb(at, "xnb", [P, MT, D])
        xb = sb(at, "xb", [KH, 2, SEQ])
        v = sb(at, "v", [P, MT, DI])
        qT = [sb(at, f"qT{i}", [P, SEQ]) for i in range(2)]
        kz = [[sb(at, f"kz{i}{j}", [P, SEQ]) for j in range(2)] for i in range(2)]
        pr = [sb(at, f"pr{i}", [P, MT, SEQ]) for i in range(2)]
        pT = [sb(at, f"pT{i}", [P, MT, SEQ]) for i in range(2)]
        nmax = sb(at, "nmax", [P, 2, MT])
        rsum = sb(at, "rsum", [P, 2, MT])
        rinv = sb(at, "rinv", [P, 2, MT])
        oT = sb(at, "oT", [P, NPAIR, SEQ])
        at.close()

        mo = ExitStack()
        xn = [sb(mo, f"xn{c}", [P, NT, ROW]) for c in range(2)]
        st = sb(mo, "st", [P, 4, D])
        xt = sb(mo, "xt", [KH, 2, 4 * P])
        logits = sb(mo, "logits", [P, NT, E])
        mx8 = sb(mo, "mx8", [P, NT, 8])
        ix8 = sb(mo, "ix8", [P, NT, 8], U32)
        ixf = sb(mo, "ixf", [P, 2, NT])
        eo = sb(mo, "eo", [P, E, NT])
        kp = sb(mo, "kp", [P, E * NT])
        bn = sb(mo, "bn", [1, NBLK_LOADED, E])
        m01 = sb(mo, "m01", [P, 2, E, NT])
        msum = sb(mo, "msum", [P, E * NT])
        tot = sb(mo, "tot", [P, E * NT])
        inc = sb(mo, "inc", [P, E * NT])
        nbi = sb(mo, "nbi", [P, E], I32)
        nbf = sb(mo, "nbf", [P, E])
        binc = sb(mo, "binc", [P, E])
        base = sb(mo, "base", [P, E])
        slotf = sb(mo, "slotf", [P, 2, NT])
        sloti = sb(mo, "sloti", [P, 2, NT], I32)
        wts = sb(mo, "wts", [P, 2, NT])
        tmp = sb(mo, "tmp", [P, E * NT])
        bcmp = sb(mo, "bcmp", [1, NBLK_LOADED, E])
        bexf = sb(mo, "bexf", [1, NBLK_LOADED])
        bex = sb(mo, "bex", [1, NBLK_LOADED], I32)
        xr = [sb(mo, f"xr{u}", [P, ROW]) for u in range(2)]
        dst = [sb(mo, f"dst{u}", [P, 2]) for u in range(2)]
        dst_next = [sb(mo, f"dst_next{u}", [P, 2]) for u in range(2)]
        dest = sb(mo, "dest", [P, 2, NT], I32)
        xT = [sb(mo, f"xT{u}", [KH + 1, 2, P]) for u in range(2)]
        hs = sb(mo, "hs", [P, F])
        hT = sb(mo, "hT", [P, FT, P])
        yv = [sb(mo, f"yv{u}", [P, D]) for u in range(2)]
        zc = [[sb(mo, f"z{c}{u}", [P, MT, D]) for u in range(2)] for c in range(2)]
        mo.close()

        bank = [ctx.enter_context(nc.psum_tensor(f"bank{i}", [P, 512], F32)) for i in range(8)]

        s_idx, s_const, s_g, s_i2, s_tokw, s_txt, s_moew = map(sem, (
            "indices_loaded", "constants_loaded", "patches_gathered", "level2_index_ready",
            "tokenizer_weights_loaded", "text_loaded", "expert_weights_loaded"))
        s_attw, s_xginit = sem("attention_weights_loaded"), sem("slots_initialised")
        s_setup = sem("constants_set")
        t_grp = sem("patches_regrouped")
        t_pe, t_ev, t_h = sem("tokenizer_product_ready"), sem("tokenizer_product_copied"), sem("image_tokens_ready")
        ln_chain, ln_var, ln_std, ln_rstd = sem("ln_dve_step"), sem("variances_ready"), sem("std_ready"), sem("rstd_ready")
        a_xn = sem("batch_normalised")
        x_full = [sem("projection0_ready"), sem("projection1_ready")]
        x_free = [sem("projection0_copied"), sem("projection1_copied")]
        s_full, s_max, exp_done = sem("scores_ready"), sem("max_ready"), [sem(f"exp_done{m}") for m in range(MT)]
        r_ready, p_ready, p_free = sem("sum_inverted"), sem("probs_ready"), [sem("probs0_used"), sem("probs1_used")]
        t_full, t_free = sem("probs_transposed"), [sem("transpose0_copied"), sem("transpose1_copied")]
        o_full, o_free = sem("head_pair_ready"), sem("head_pair_copied")
        h_done = sem("attention_added")
        r_ln, r_copy, r_T, r_Tev, r_log, r_logev = map(sem, (
            "router_input_ready", "routed_rows_copied", "router_input_transposed", "router_transpose_copied",
            "logits_ready", "logits_copied"))
        r_chain, r_d, r_e, r_m, r_cnt, r_slot, r_blk = map(sem, (
            "router_dve_step", "logit_gap_ready", "gap_exp_ready", "choice_masks_ready", "ranks_ready", "slots_ready",
            "block_experts_ready"))
        s_scat = sem("rows_scattered")
        b_load = [sem("block_loaded0"), sem("block_loaded1")]
        b_x, b_xev, b_h, b_g, b_t, b_tev, b_y, b_yev, b_yw = map(sem, (
            "block_transposed", "block_transpose_copied", "hidden_ready", "gelu_done", "hidden_transposed",
            "hidden_transpose_copied", "expert_out_ready", "expert_bias_added", "expert_out_weighted"))
        b_addr, b_dst = sem("next_addresses_copied"), sem("addresses_ready")
        y_free = [sem("result0_free"), sem("result1_free")]
        b_scat = [sem("result_scattered0"), sem("result_scattered1")]
        z_load = [sem("results_loaded0"), sem("results_loaded1")]
        z_chain, z_sum, z_out = sem("first_result_added"), sem("output_tile_ready"), sem("output_stored")

        primed = [*x_free, *exp_done, *p_free, *t_free, o_free, r_T, r_Tev, r_logev, r_copy, b_xev, b_tev, b_yev, *y_free]

        block = ctx.enter_context(nc.Block())
        h_flat = h[:].rearrange("p t d -> p (t d)")

        @block.sync
        def _(sp):
            sp.dma_start(i0[:], idx0.rearrange("(a t i) -> t a i", a=2, i=GP)).then_inc(s_idx, 16)
            sp.dma_start(i1[:], idx1.rearrange("(t i) -> t i", i=GP)).then_inc(s_idx, 16)
            for b in range(B):
                sp.dma_start(i2[16 * b:16 * b + 16, :], idx2.rearrange("(t i) -> t i", i=GP)).then_inc(s_idx, 16)
            sp.dma_start(i2b[:], base2).then_inc(s_idx, 16)
            for dst_, src in ((ident, ident_c), (tri, tri_c), (wr, WrT)):
                sp.dma_start(dst_[:], src).then_inc(s_const, 16)
            for dst_, src in ((w0, W0T), (w1, W1T), (w2, W2T), (a1, A1), (a2, A2)):
                sp.dma_start(dst_[:], src).then_inc(s_tokw, 16)
            sp.dma_start(wfa[:], WfT[0:P, :]).then_inc(s_tokw, 16)
            sp.dma_start(wfb[:], WfT[P:D, :]).then_inc(s_tokw, 16)
            sp.dma_start(bca[0:EMB, :], b0).then_inc(s_tokw, 16)
            sp.dma_start(bca[EMB:P, :], b1).then_inc(s_tokw, 16)
            sp.dma_start(bcb[:], b2).then_inc(s_tokw, 16)
            sp.dma_start(bf_bc[:], bf.broadcast_to([P, D])).then_inc(s_tokw, 16)
            for b in range(B):
                sp.dma_start(h[:, b * MT + 2, :], txt[b]).then_inc(s_txt, 16)
            sp.dma_start(wi[0:KH, :, :], WiT).then_inc(s_moew, 16)
            sp.dma_start(wi[KH:KH + 1, 1, :], bi).then_inc(s_moew, 16)
            sp.dma_start(wo2[:], WoT).then_inc(s_moew, 16)
            sp.dma_start(bo_bc[:], bo.broadcast_to([P, E * D])).then_inc(s_moew, 16)
            sp.dma_start(xg, xg_init).then_inc(s_xginit, 16)
            sp.wait_ge(t_h, 16)
            sp.dma_start(wq[:], wqkv).then_inc(s_attw, 16)
            sp.dma_start(wot[:], wo).then_inc(s_attw, 16)
            sp.wait_ge(h_done, B * MT)
            sp.dma_start(eo[:], expert_of).then_inc(s_attw, 16)
            sp.dma_start(kp[:], keep).then_inc(s_attw, 16)
            sp.dma_start(bn[:], block_no).then_inc(s_attw, 16)
            sp.dma_start(dest[:], dest_c).then_inc(s_attw, 16)
            sp.wait_ge(s_scat, 16 * 2 * NT)
            for u in range(2):
                sp.dma_start(xr[u][:], xg[u * P:(u + 1) * P, :]).then_inc(b_load[u], 16)
            with sp.Fori(0, NBLK // 2) as i:
                for u in range(2):
                    sp.wait_ge(b_x, 2 * i + u + 1)
                    sp.wait_ge(b_addr, 2 * i + u + 1)
                    sp.dma_start(xr[u][:], xg[bass.ds((2 * i + 2 + u) * P, P), :]).then_inc(b_load[u], 16)
            for u in range(2):
                sp.wait_ge(b_scat[u], 16 * (NBLK // 2))
                sp.wait_ge(b_load[u], 16 * (NBLK // 2 + 1))
            sp.wait_ge(b_x, NBLK + 2)
            for b in range(B):
                if b >= 2:
                    sp.wait_ge(z_sum, b - 1)
                    sp.wait_ge(z_out, 16 * (b - 1))
                for c in range(2):
                    src = z[c * NTOK + b * SEQ:c * NTOK + (b + 1) * SEQ, :].rearrange("(m p) d -> p m d", p=P)
                    sp.dma_start(zc[c][b % 2][:], src).then_inc(z_load[b % 2], 16)
                if b >= 1:
                    sp.wait_ge(z_sum, b)
                    sp.dma_start(out[b - 1].rearrange("(m p) d -> p m d", p=P), h[:, (b - 1) * MT:b * MT, :]).then_inc(z_out, 16)
            sp.wait_ge(z_sum, B)
            sp.dma_start(out[B - 1].rearrange("(m p) d -> p m d", p=P), h[:, (B - 1) * MT:B * MT, :]).then_inc(z_out, 16)
            sp.wait_ge(z_out, 16 * B)

        @block.gpsimd
        def _(pool):
            for s in primed:
                pool.sem_inc(s, PRIMED)
            pool.memset(ones[:], 1.0).then_inc(s_setup, 1)
            pool.memset(epsc[:], EPS).then_inc(s_setup, 1)
            pool.wait_ge(s_idx, 16 * (B + 3))
            pool.tensor_tensor(i2[:], i2[:], i2b[:], ALU.add).then_inc(s_i2, 1)
            for i in range(GP):
                for a in range(2):
                    pool.indirect_dma_start(out=g0[:, a, i, :], out_offset=None, in_=xp0,
                                            in_offset=bass.IndirectOffsetOnAxis(ap=i0[:, a, i:i + 1], axis=0)).then_inc(s_g, 16)
                pool.indirect_dma_start(out=g1[:, i, :], out_offset=None, in_=xp1,
                                        in_offset=bass.IndirectOffsetOnAxis(ap=i1[:, i:i + 1], axis=0)).then_inc(s_g, 16)
            pool.wait_ge(s_i2, 1)
            for i in range(GP):
                pool.indirect_dma_start(out=g2[:, i, :], out_offset=None, in_=xp2,
                                        in_offset=bass.IndirectOffsetOnAxis(ap=i2[:, i:i + 1], axis=0)).then_inc(s_g, 16)
            pool.wait_ge(t_h, 16)
            for i in range(2):
                pool.memset(kz[i][0][DH:P, :], 0.0).then_inc(s_setup, 1)
                pool.memset(kz[i][1][0:DH, :], 0.0).then_inc(s_setup, 1)
            pool.wait_ge(h_done, B * MT)
            for u in range(2):
                pool.memset(xT[u][KH:KH + 1, 1, :], 1.0).then_inc(s_setup, 1)
            pool.wait_ge(s_xginit, 16)
            pool.wait_ge(r_slot, 1)
            pool.wait_ge(r_ln, 6)
            pool.wait_ge(r_copy, 6 + PRIMED)
            for c in range(2):
                for t in range(NT):
                    pool.indirect_dma_start(out=xg, out_offset=bass.IndirectOffsetOnAxis(ap=sloti[:, c, t:t + 1], axis=0),
                                            in_=xn[c][:, t, :], in_offset=None).then_inc(s_scat, 16)
            with pool.Fori(0, NBLK // 2) as i:
                for u in range(2):
                    pool.wait_ge(b_yw, 2 * i + u + 1)
                    pool.nop(nofuse=True)
                    pool.indirect_dma_start(out=z, out_offset=bass.IndirectOffsetOnAxis(ap=dst[u][:, 0:1].bitcast(I32), axis=0),
                                            in_=yv[u][:], in_offset=None).then_inc(b_scat[u], 16)
                    pool.wait_ge(b_scat[u], 16 * (i + 1))
                    pool.sem_inc(y_free[u], 1)

        @block.tensor
        def _(pe):
            pe.wait_ge(s_const, 48)
            pe.wait_ge(s_g, 16 * 4 * GP)
            pe.wait_ge(t_grp, 3)
            k = 0

            def start_product(first):
                if first >= 4:
                    pe.wait_ge(t_ev, first - 3)
            for b in range(0, B, 2):
                start_product(k)
                for j in range(4):
                    last = pe.transpose(bank[k % 4][0:48, j * P:(j + 1) * P],
                                        g0b[:, j % 2, b + j // 2, :], ident[:])
                last.then_inc(t_pe, 1)
                k += 1
            for kt in range(2):
                start_product(k)
                for b in range(B):
                    last = pe.transpose(bank[k % 4][0:96, b * 64:(b + 1) * 64],
                                        g1b[:, b, kt * 96:(kt + 1) * 96], ident[0:64, 0:64])
                last.then_inc(t_pe, 1)
                k += 1
            for kt in range(2):
                start_product(k)
                for j in range(4):
                    last = pe.transpose(bank[k % 4][0:96, j * P:(j + 1) * P],
                                        g2[:, (kt * 4 + j) * 2:(kt * 4 + j) * 2 + 2, :].rearrange("p i c -> p (i c)"), ident[:])
                last.then_inc(t_pe, 1)
                k += 1
            pe.wait_ge(s_tokw, 16 * 11)
            pe.wait_ge(t_ev, 6)
            for b in range(B):
                for kt in range(2):
                    last = pe.matmul(bank[k % 4][0:64, b * 64:(b + 1) * 64], g1t[:, kt, b * 64:(b + 1) * 64], w1[:, kt, :],
                                     start=kt == 0, stop=kt == 1)
            last.then_inc(t_pe, 1)
            k += 1
            pe.wait_ge(t_ev, 8)
            for kt in range(8):
                last = pe.matmul(bank[k % 4][:, 0:EMB], g2t[:, kt, :], w2[:, kt, :], start=kt == 0, stop=kt == 7)
            last.then_inc(t_pe, 1)
            k += 1
            for b in range(0, B, 2):
                start_product(k)
                pe.matmul(bank[k % 4][0:EMB, :], w0[:], g0t[:, b * TOK_IMG:(b + 2) * TOK_IMG],
                          start=True, stop=True).then_inc(t_pe, 1)
                k += 1
            for b in range(0, B, 2):
                start_product(k)
                for j in range(2):
                    last = pe.matmul(bank[k % 4][EMB:P, j * TOK_IMG:(j + 1) * TOK_IMG],
                                     e1[:, (b + j) * 64:(b + j + 1) * 64], a1[:], start=True, stop=True)
                last.then_inc(t_pe, 1)
                k += 1
            for b in range(0, B, 2):
                start_product(k)
                for j in range(2):
                    last = pe.matmul(bank[k % 4][0:EMB, j * TOK_IMG:(j + 1) * TOK_IMG],
                                     e2[:], a2[:, b + j, :], start=True, stop=True)
                last.then_inc(t_pe, 1)
                k += 1
            pe.wait_ge(t_ev, 22)
            for b in range(B):
                for a in range(2):
                    start_product(k)
                    c0 = b * TOK_IMG + a * P
                    pe.matmul(bank[k % 4][:, 0:D], ya[:, c0:c0 + P], wfa[:], start=True, stop=False)
                    pe.matmul(bank[k % 4][:, 0:D], yb[:, c0:c0 + P], wfb[:], start=False, stop=True).then_inc(t_pe, 1)
                    k += 1

            PB = [bank[0], bank[1]]
            SB = bank[2:5]
            TB = bank[5:7]
            OB = bank[7]
            pe.wait_ge(s_attw, 32)
            pe.wait_ge(s_setup, 6)
            with pe.Fori(0, B) as b:
                n_in = [0, 0]

                def fill(j):
                    pe.wait_ge(x_free[j], b * (12 - j) + n_in[j] + PRIMED)
                    n_in[j] += 1
                    return PB[j]

                pe.wait_ge(a_xn, b + 1)
                for kt in range(2):
                    o = fill(kt)
                    for m in range(MT):
                        last = pe.transpose(o[0:KH, m * P:(m + 1) * P], xnb[:, m, kt * KH:(kt + 1) * KH], ident[:])
                    last.then_inc(x_full[kt], 1)
                for j in range(2):
                    pe.wait_ge(x_free[j], b * (12 - j) + 1 + PRIMED)
                for m in range(MT):
                    for j in range(2):
                        o = fill(j)
                        for kt in range(2):
                            last = pe.matmul(o[:, 0:384], xb[:, kt, m * P:(m + 1) * P],
                                             wq[:, kt, 2 * DI + j * 384:2 * DI + (j + 1) * 384], start=kt == 0, stop=kt == 1)
                        last.then_inc(x_full[j], 1)

                def project(p):
                    for j in range(2):
                        o = fill(j)
                        for kt in range(2):
                            last = pe.matmul(o[:, 0:SEQ], wq[:, kt, j * DI + p * P:j * DI + (p + 1) * P], xb[:, kt, :],
                                             start=kt == 0, stop=kt == 1)
                        last.then_inc(x_full[j], 1)

                def score(n):
                    p = n // 2
                    if n % 2 == 0:
                        pe.wait_ge(x_free[0], b * 12 + 4 + p + 1 + PRIMED)
                        pe.wait_ge(x_free[1], b * 11 + 4 + p + 1 + PRIMED)
                    for m in range(MT):
                        pe.wait_ge(exp_done[m], b * HEADS + n + PRIMED)
                        pe.matmul(SB[m][:, 0:SEQ], qT[p % 2][:, m * P:(m + 1) * P], kz[p % 2][n % 2][:],
                                  start=True, stop=True).then_inc(s_full, 1)

                project(0)
                score(0)
                for n in range(HEADS):
                    p = n // 2
                    if n % 2 == 0 and p + 1 < NPAIR:
                        project(p + 1)
                    if n + 1 < HEADS:
                        score(n + 1)
                    pe.wait_ge(p_ready, b * HEADS + n + 1)
                    for j in range(MT):
                        e = n * MT + j
                        pe.wait_ge(t_free[e % 2], b * (HEADS * MT // 2) + e // 2 + PRIMED)
                        for m in range(MT):
                            last = pe.transpose(TB[e % 2][:, m * P:(m + 1) * P], pr[n % 2][:, m, j * P:(j + 1) * P], ident[:])
                        last.then_inc(t_full, 1)
                    if n % 2 == 0:
                        pe.wait_ge(o_free, b * NPAIR + p + PRIMED)
                    for j in range(MT):
                        e = n * MT + j
                        pe.wait_ge(t_free[e % 2], b * (HEADS * MT // 2) + e // 2 + 1 + PRIMED)
                        last = pe.matmul(OB[(n % 2) * DH:(n % 2) * DH + DH, 0:SEQ], v[:, j, n * DH:(n + 1) * DH],
                                         pT[n % 2][:, j, :], start=j == 0, stop=j == MT - 1)
                        if j == 0:
                            last.then_inc(p_free[n % 2], 1)
                    if n % 2 == 1:
                        last.then_inc(o_full, 1)
                pe.wait_ge(o_free, b * NPAIR + NPAIR + PRIMED)
                for m in range(MT):
                    o = fill(m % 2)
                    for p in range(NPAIR):
                        last = pe.matmul(o[:, 0:D], oT[:, p, m * P:(m + 1) * P], wot[:, p, :], start=p == 0, stop=p == NPAIR - 1)
                    last.then_inc(x_full[m % 2], 1)

            pe.wait_ge(h_done, B * MT)
            with pe.Fori(0, NT // 4) as g:
                pe.wait_ge(r_ln, g + 1)
                pe.wait_ge(r_Tev, 2 * g + PRIMED)
                for kt in range(2):
                    for j in range(4):
                        last = pe.transpose(bank[kt][0:KH, j * P:(j + 1) * P], st[:, j, kt * KH:(kt + 1) * KH], ident[:])
                    last.then_inc(r_T, 1)
                pe.wait_ge(r_Tev, 2 * g + 2 + PRIMED)
                pe.wait_ge(r_logev, g + PRIMED)
                for j in range(4):
                    for kt in range(2):
                        last = pe.matmul(bank[2][:, j * E:(j + 1) * E], xt[:, kt, j * P:(j + 1) * P], wr[:, kt, :],
                                         start=kt == 0, stop=kt == 1)
                last.then_inc(r_log, 1)
            pe.wait_ge(r_m, 1)
            pe.matmul(bank[0][:, 0:E * NT], tri[:], msum[:], start=True, stop=True)
            pe.matmul(bank[1][:, 0:E * NT], ones[:], msum[:], start=True, stop=True).then_inc(r_cnt, 1)

            HB, TT, YB, XB = bank[0:2], bank[2:4], bank[4:6], bank[6]

            def block_transpose(n, u):
                pe.wait_ge(b_load[u], 16 * ((n - u) // 2 + 1) if isinstance(n, int) else 8 * (n - u) + 16)
                pe.wait_ge(b_xev, n + PRIMED)
                for kt in range(2):
                    last = pe.transpose(XB[0:KH, kt * P:(kt + 1) * P], xr[u][:, kt * KH:(kt + 1) * KH], ident[:])
                last.then_inc(b_x, 1)

            def hidden(n, u, expert):
                pe.wait_ge(b_xev, n + 1 + PRIMED)
                for f in range(2):
                    cols = bass.ds(expert * F + f * FH, FH)
                    pe.matmul(HB[f][:, 0:FH], xT[u][0:KH, 0, :], wi[0:KH, 0, cols], start=True, stop=False)
                    pe.matmul(HB[f][:, 0:FH], xT[u][:, 1, :], wi[:, 1, cols], start=False, stop=True).then_inc(b_h, 1)

            def expert_of_block(n):
                return pe.value_load(bex[0:1, bass.ds(n, 1)], min_val=0, max_val=E - 1)

            pe.wait_ge(s_moew, 64)
            pe.wait_ge(s_setup, 8)
            pe.wait_ge(r_blk, 1)
            block_transpose(0, 0)
            block_transpose(1, 1)
            hidden(0, 0, expert_of_block(0))
            with pe.Fori(0, NBLK // 2) as i:
                ex = [expert_of_block(2 * i + u) for u in range(3)]
                for u in range(2):
                    n = 2 * i + u
                    for f in range(2):
                        pe.wait_ge(b_g, 2 * n + f + 1)
                        pe.wait_ge(b_tev, 2 * n + PRIMED)
                        for j in range(3):
                            last = pe.transpose(TT[f][:, j * P:(j + 1) * P], hs[:, (3 * f + j) * P:(3 * f + j + 1) * P], ident[:])
                        last.then_inc(b_t, 1)
                    block_transpose(n + 2, u)
                    hidden(n + 1, 1 - u, ex[u + 1])
                    pe.wait_ge(b_yev, n + PRIMED)
                    for j in range(FT):
                        if j % 3 == 0:
                            pe.wait_ge(b_tev, 2 * n + j // 3 + 1 + PRIMED)
                        last = pe.matmul(YB[u][:, 0:D], hT[:, j, :], wo2[:, bass.ds(ex[u] * FT + j, 1), :].rearrange("p o d -> p (o d)"),
                                         start=j == 0, stop=j == FT - 1)
                    last.then_inc(b_y, 1)

        @block.scalar
        def _(act):
            def tok_copy(k, out_, in_, bias=None):
                act.wait_ge(t_pe, k + 1)
                act.wait_ge(t_ev, k)
                if bias is None:
                    act.activation(out_, in_, ACT.Copy).then_inc(t_ev, 1)
                else:
                    act.activation(out_, in_, ACT.Identity, bias=bias).then_inc(t_ev, 1)

            act.wait_ge(s_tokw, 16 * 11)
            k = 0
            for j in range(4):
                tok_copy(k, g0t[:, j * 512:(j + 1) * 512], bank[k % 4][0:48, :])
                k += 1
            for kt in range(2):
                tok_copy(k, g1t[:, kt, :], bank[k % 4][0:96, :])
                k += 1
            for kt in range(2):
                tok_copy(k, g2t[:, kt * 4:(kt + 1) * 4, :].rearrange("p a b -> p (a b)"), bank[k % 4][0:96, :])
                k += 1
            tok_copy(k, e1[:], bank[k % 4][0:64, :])
            k += 1
            tok_copy(k, e2[:], bank[k % 4][:, 0:EMB])
            k += 1
            for j in range(4):
                tok_copy(k, ya[0:EMB, j * 512:(j + 1) * 512], bank[k % 4][0:EMB, :], bca[0:EMB, :])
                k += 1
            for j in range(4):
                tok_copy(k, ya[EMB:P, j * 512:(j + 1) * 512], bank[k % 4][EMB:P, :], bca[EMB:P, :])
                k += 1
            for j in range(4):
                tok_copy(k, yb[:, j * 512:(j + 1) * 512], bank[k % 4][0:EMB, :], bcb[:])
                k += 1
            act.wait_ge(s_setup, 2)
            act.wait_ge(ln_var, 1)
            act.activation(rstd[:], mv[:, :, 1], ACT.Sqrt, bias=epsc[:]).then_inc(ln_std, 1)

            with act.Fori(0, B) as b:
                n_out = [0, 0]

                def drain_bank(j, out_, in_, scale=None):
                    act.wait_ge(x_full[j], b * (12 - j) + n_out[j] + 1)
                    if scale is None:
                        act.activation(out_, in_, ACT.Copy).then_inc(x_free[j], 1)
                    else:
                        act.activation(out_, in_, ACT.Copy, scale=scale).then_inc(x_free[j], 1)
                    n_out[j] += 1

                drain_bank(0, xb[:, 0, :], bank[0][0:KH, 0:SEQ])
                for m in range(MT):
                    drain_bank(0, v[:, m, 0:384], bank[0][:, 0:384])

                def exps(n):
                    if n % 2 == 0:
                        drain_bank(0, qT[(n // 2) % 2][:], bank[0][:, 0:SEQ], DH ** -0.5)
                    act.wait_ge(p_free[n % 2], b * (HEADS // 2) + n // 2 + PRIMED)
                    for m in range(MT):
                        act.wait_ge(s_max, b * HEADS * MT + n * MT + m + 1)
                        act.activation(pr[n % 2][:, m, :], bank[2 + m][:, 0:SEQ], ACT.Exp, bias=nmax[:, n % 2, m:m + 1],
                                       accum_out=rsum[:, n % 2, m:m + 1]).then_inc(exp_done[m], 1)

                for n in range(HEADS):
                    exps(n)

            act.wait_ge(ln_var, 2)
            act.activation(rstd[:], mv[:, :, 1], ACT.Sqrt, bias=epsc[:]).then_inc(ln_std, 1)
            with act.Fori(0, NT // 4) as g:
                act.wait_ge(r_T, 2 * g + 1 + PRIMED)
                act.activation(xt[:, 0, :], bank[0][0:KH, :], ACT.Copy).then_inc(r_Tev, 1)
                act.wait_ge(r_ln, g + 1)
                for c in range(2):
                    last = act.activation(xn[c][:, bass.ds(g * 4, 4), 0:D], st[:], ACT.Copy)
                last.then_inc(r_copy, 1)
            act.wait_ge(r_d, 1)
            act.activation(wts[:, 1, :], wts[:, 0, :], ACT.Exp).then_inc(r_e, 1)
            for f in range(2):
                act.wait_ge(b_h, f + 1)
                act.activation(hs[:, f * FH:(f + 1) * FH], bank[f][:, 0:FH], ACT.Gelu).then_inc(b_g, 1)
            with act.Fori(0, NBLK // 2) as i:
                for u in range(2):
                    for f in range(2):
                        act.wait_ge(b_h, 4 * i + 2 * u + f + 3)
                        act.activation(hs[:, f * FH:(f + 1) * FH], bank[f][:, 0:FH], ACT.Gelu).then_inc(b_g, 1)

        @block.vector
        def _(dve):
            dve.wait_ge(s_g, 16 * 4 * GP)
            for a in range(2):
                dve.tensor_copy(g0b[:, a].rearrange("p b (i c) -> p i b c", c=3),
                                g0[:, a].rearrange("p i (b c) -> p i b c", c=3)).then_inc(t_grp, 1)
            dve.tensor_copy(g1b[:].rearrange("p b (i c) -> p i b c", c=12),
                            g1[:].rearrange("p i (b c) -> p i b c", c=12)).then_inc(t_grp, 1)
            dve.wait_ge(s_tokw, 16 * 11)
            k = 22
            for b in range(B):
                for a in range(2):
                    dve.wait_ge(t_pe, k + 1)
                    dve.tensor_tensor(h[:, b * MT + a, :], bank[k % 4][:, 0:D], bf_bc[:], ALU.add).then_inc(t_ev, 1)
                    k += 1
            dve.wait_ge(t_ev, 38)
            dve.engine_nop().then_inc(t_h, 16)

            def layer_stats(done):
                for t in range(NT):
                    last = dve.bn_stats(stats[:, t, :], h[:, t, :])
                last.then_inc(ln_chain, 1)
                dve.wait_ge(ln_chain, done)
                for t in range(NT):
                    last = dve.bn_aggr(mv[:, t, :], stats[:, t, :])
                last.then_inc(ln_var, 1)
                dve.wait_ge(ln_var, done)

            dve.wait_ge(s_txt, 16 * B)
            layer_stats(1)
            dve.wait_ge(ln_std, 1)
            dve.reciprocal(rstd[:], rstd[:]).then_inc(ln_rstd, 1)
            dve.wait_ge(ln_rstd, 1)

            with dve.Fori(0, B) as b:
                n_out = [0, 0]

                def full(j):
                    dve.wait_ge(x_full[j], b * (12 - j) + n_out[j] + 1)
                    n_out[j] += 1

                for m in range(MT):
                    t = b * MT + m
                    last = dve.tensor_scalar(xnb[:, m, :], h_flat[:, bass.ds(t * D, D)], mv[:, bass.ds(t, 1), 0:1].rearrange("p o d -> p (o d)"),
                                             rstd[:, bass.ds(t, 1)], ALU.subtract, ALU.mult)
                last.then_inc(a_xn, 1)
                full(1)
                dve.tensor_copy(xb[:, 1, :], bank[1][0:KH, 0:SEQ]).then_inc(x_free[1], 1)
                for m in range(MT):
                    full(1)
                    dve.tensor_copy(v[:, m, 384:768], bank[1][:, 0:384]).then_inc(x_free[1], 1)

                def keys(p):
                    full(1)
                    dve.tensor_copy(kz[p % 2][0][0:DH, :], bank[1][0:DH, 0:SEQ])
                    dve.tensor_copy(kz[p % 2][1][DH:P, :], bank[1][DH:P, 0:SEQ]).then_inc(x_free[1], 1)

                def maxes(n):
                    for m in range(MT):
                        dve.wait_ge(s_full, b * HEADS * MT + n * MT + m + 1)
                        dve.tensor_reduce(nmax[:, n % 2, m:m + 1], bank[2 + m][:, 0:SEQ], AX_X, ALU.max, negate=True).then_inc(s_max, 1)

                def normalise(n):
                    for m in range(MT):
                        dve.wait_ge(exp_done[m], b * HEADS + n + 1 + PRIMED)
                    dve.reciprocal(rinv[:, n % 2, :], rsum[:, n % 2, :]).then_inc(r_ready, 1)
                    dve.wait_ge(r_ready, b * HEADS + n + 1)
                    for m in range(MT):
                        last = dve.tensor_scalar(pr[n % 2][:, m, :], pr[n % 2][:, m, :], rinv[:, n % 2, m:m + 1], None, ALU.mult)
                    last.then_inc(p_ready, 1)

                keys(0)
                maxes(0)
                normalise(0)
                for n in range(HEADS):
                    p = n // 2
                    if n % 2 == 0 and p + 1 < NPAIR:
                        keys(p + 1)
                    if n + 1 < HEADS:
                        maxes(n + 1)
                    for j in range(MT):
                        e = n * MT + j
                        dve.wait_ge(t_full, b * HEADS * MT + e + 1)
                        dve.tensor_copy(pT[n % 2][:, j, :], bank[5 + e % 2][:, 0:SEQ]).then_inc(t_free[e % 2], 1)
                    if n + 1 < HEADS:
                        normalise(n + 1)
                    if n % 2 == 1:
                        dve.wait_ge(o_full, b * NPAIR + p + 1)
                        dve.tensor_copy(oT[:, p, :], bank[7][:, 0:SEQ]).then_inc(o_free, 1)
                n_out[0] = 10
                for m in range(MT):
                    full(m % 2)
                    t = b * MT + m
                    dst_ = h_flat[:, bass.ds(t * D, D)]
                    dve.tensor_tensor(dst_, dst_, bank[m % 2][:, 0:D], ALU.add).then_inc(x_free[m % 2], 1)
                dve.wait_ge(x_free[0], b * 12 + 12 + PRIMED)
                dve.wait_ge(x_free[1], b * 11 + 11 + PRIMED)
                dve.engine_nop().then_inc(h_done, MT)

            layer_stats(2)
            dve.wait_ge(ln_std, 2)
            dve.reciprocal(rstd[:], rstd[:]).then_inc(ln_rstd, 1)
            dve.wait_ge(ln_rstd, 2)
            with dve.Fori(0, NT // 4) as g:
                dve.wait_ge(r_T, 2 * g + PRIMED)
                dve.wait_ge(r_copy, g + PRIMED)
                for j in range(4):
                    t = g * 4 + j
                    last = dve.tensor_scalar(st[:, j, :], h_flat[:, bass.ds(t * D, D)], mv[:, bass.ds(t, 1), 0:1].rearrange("p o d -> p (o d)"),
                                             rstd[:, bass.ds(t, 1)], ALU.subtract, ALU.mult)
                last.then_inc(r_ln, 1)
                dve.wait_ge(r_T, 2 * g + 2 + PRIMED)
                dve.tensor_copy(xt[:, 1, :], bank[1][0:KH, :]).then_inc(r_Tev, 1)
                dve.wait_ge(r_log, g + 1)
                dve.tensor_copy(logits[:, bass.ds(g * 4, 4), :].rearrange("p t e -> p (t e)"), bank[2][:, 0:4 * E]).then_inc(r_logev, 1)
            dve.wait_ge(r_logev, NT // 4 + PRIMED)

            steps = [0]

            def step(instruction):
                steps[0] += 1
                instruction.then_inc(r_chain, 1)
                dve.wait_ge(r_chain, steps[0])

            for t in range(NT):
                last = dve.max(mx8[:, t, :], logits[:, t, :])
            step(last)
            for t in range(NT):
                last = dve.max_index(ix8[:, t, :], mx8[:, t, :], logits[:, t, :])
            step(last)
            dve.tensor_tensor(wts[:, 0, :], mx8[:, :, 1], mx8[:, :, 0], ALU.subtract).then_inc(r_d, 1)
            dve.wait_ge(s_attw, 16 * 6)
            for c in range(2):
                last = dve.tensor_copy(ixf[:, c, :], ix8[:, :, c])
            step(last)
            for c in range(2):
                last = dve.tensor_tensor(m01[:, c], eo[:], ixf[:, c:c + 1, :].broadcast_to([P, E, NT]), ALU.is_equal)
            step(last)
            dve.tensor_tensor(msum[:], m01[:, 0].rearrange("p e t -> p (e t)"), m01[:, 1].rearrange("p e t -> p (e t)"), ALU.add).then_inc(r_m, 1)
            dve.wait_ge(r_e, 1)
            step(dve.tensor_scalar(wts[:, 0, :], wts[:, 1, :], 1.0, None, ALU.add))
            step(dve.reciprocal(wts[:, 0, :], wts[:, 0, :]))
            step(dve.tensor_tensor(wts[:, 1, :], wts[:, 1, :], wts[:, 0, :], ALU.mult))
            for c in range(2):
                dve.tensor_copy(xn[c][:, :, D + 1], wts[:, c, :])
                last = dve.tensor_copy(xn[c][:, :, D].bitcast(I32), dest[:, c, :])
            step(last)
            dve.wait_ge(r_cnt, 1)
            step(dve.tensor_copy(tot[:], bank[1][:, 0:E * NT]))
            step(dve.tensor_tensor_scan(inc[:], kp[:], tot[:], 0.0, ALU.mult, ALU.add))
            n_e = inc[:].rearrange("p (e t) -> p e t", e=E)[:, :, NT - 1]
            step(dve.tensor_scalar(nbi[:], n_e, float(P - 1), None, ALU.add))
            step(dve.tensor_scalar(nbi[:], nbi[:], 7, None, ALU.logical_shift_right))
            step(dve.tensor_copy(nbf[:], nbi[:]))
            step(dve.tensor_tensor_scan(binc[:], ones[:, 0:E], nbf[:], 0.0, ALU.mult, ALU.add))
            step(dve.tensor_tensor(base[:], binc[:], nbf[:], ALU.subtract))
            step(dve.tensor_scalar(base[:], base[:], float(P), None, ALU.mult))
            step(dve.tensor_tensor(inc[:], inc[:], tot[:], ALU.subtract))
            step(dve.tensor_tensor(inc[:], inc[:], bank[0][:, 0:E * NT], ALU.add))
            inc3 = inc[:].rearrange("p (e t) -> p e t", e=E)
            step(dve.tensor_tensor(inc3, inc3, base[:].rearrange("p (e o) -> p e o", o=1).broadcast_to([P, E, NT]), ALU.add))
            for c in range(2):
                step(dve.tensor_tensor(tmp[:], inc[:], m01[:, c].rearrange("p e t -> p (e t)"), ALU.mult))
                step(dve.tensor_reduce(slotf[:, c, :], tmp[:].rearrange("p (e t) -> p t e", e=E), AX_X, ALU.add))
            dve.tensor_copy(sloti[:], slotf[:]).then_inc(r_slot, 1)
            step(dve.tensor_tensor(bcmp[:], binc[0:1, :].rearrange("p (o e) -> p o e", o=1).broadcast_to([1, NBLK_LOADED, E]), bn[:], ALU.is_le))
            step(dve.tensor_reduce(bexf[:], bcmp[:], AX_X, ALU.add))
            step(dve.tensor_scalar(bexf[:], bexf[:], float(E - 1), None, ALU.min))
            step(dve.tensor_copy(bex[:], bexf[:]))
            dve.engine_nop().then_inc(r_blk, 1)

            def block_copy(u, it):
                dve.wait_ge(b_x, 2 * it + u + 1)
                dve.tensor_copy(xT[u][0:KH, :, :], bank[6][0:KH, 0:2 * P].rearrange("p (k n) -> p k n", k=2)).then_inc(b_xev, 1)

            def address_copy(u, it):
                dve.wait_ge(b_load[u], 16 * (it + 1))
                dve.tensor_copy(dst_next[u][:].bitcast(I32), xr[u][:, D:ROW].bitcast(I32)).then_inc(b_addr, 1)

            dve.wait_ge(s_moew, 64)
            for u in range(2):
                block_copy(u, 0)
                address_copy(u, 0)
            with dve.Fori(0, NBLK // 2) as i:
                ex = [dve.value_load(bex[0:1, bass.ds(2 * i + u, 1)], min_val=0, max_val=E - 1) for u in range(2)]
                for u in range(2):
                    for f in range(2):
                        dve.wait_ge(b_t, 4 * i + 2 * u + f + 1)
                        dve.tensor_copy(hT[:, 3 * f:3 * f + 3, :].rearrange("p a b -> p (a b)"), bank[2 + f][:, 0:FH]).then_inc(b_tev, 1)
                    block_copy(u, i + 1)
                    dve.wait_ge(y_free[u], i + PRIMED)
                    dve.wait_ge(b_addr, 2 * i + u + 1)
                    dve.tensor_copy(dst[u][:].bitcast(I32), dst_next[u][:].bitcast(I32)).then_inc(b_dst, 1)
                    dve.wait_ge(b_y, 2 * i + u + 1)
                    dve.tensor_tensor(yv[u][:], bank[4 + u][:, 0:D], bo_bc[:, bass.ds(ex[u] * D, D)], ALU.add).then_inc(b_yev, 1)
                    dve.wait_ge(b_yev, 2 * i + u + 1 + PRIMED)
                    dve.wait_ge(b_dst, 2 * i + u + 1)
                    dve.tensor_scalar(yv[u][:], yv[u][:], dst[u][:, 1:2], None, ALU.mult).then_inc(b_yw, 1)
                    address_copy(u, i + 1)

            for b in range(B):
                dve.wait_ge(z_load[b % 2], 32 * (b // 2 + 1))
                hb = h[:, b * MT:(b + 1) * MT, :]
                dve.tensor_tensor(hb, hb, zc[0][b % 2][:], ALU.add).then_inc(z_chain, 1)
                dve.wait_ge(z_chain, b + 1)
                dve.tensor_tensor(hb, hb, zc[1][b % 2][:], ALU.add).then_inc(z_sum, 1)


def interpolation(n_in, n_out):
    pos = (np.arange(n_out, dtype=np.float32) + np.float32(0.5)) * np.float32(n_in / n_out) - np.float32(0.5)
    pos = np.clip(pos, 0.0, n_in - 1).astype(np.float32)
    lo = np.floor(pos).astype(np.int64)
    hi = np.minimum(lo + 1, n_in - 1)
    w = (pos - lo).astype(np.float32)
    m = np.zeros((n_in, n_out), np.float32)
    m[lo, np.arange(n_out)] += np.float32(1.0) - w
    m[hi, np.arange(n_out)] += w
    return m


def shape_constants():
    a1 = interpolation(64, TOK_IMG)
    a2 = interpolation(16, TOK_IMG)
    big = np.zeros((P, B, TOK_IMG), np.float32)
    for b in range(B):
        big[16 * b:16 * b + 16, b] = a2
    p = np.arange(P)
    dest = np.stack([c * NTOK + np.arange(NT)[None, :] * P + p[:, None] for c in range(2)], 1).astype(np.int32)
    xg = np.zeros((NBLK_LOADED * P, ROW), np.float32)
    xg[:, D] = (2 * NTOK + np.arange(NBLK_LOADED * P)).astype(np.int32).view(np.float32)
    return {
        "base2": np.repeat((256 * (p // 16)).astype(np.int32)[:, None], GP, 1),
        "ident_c": np.eye(P, dtype=np.float32),
        "tri_c": np.triu(np.ones((P, P), np.float32), 1),
        "A1": a1, "A2": big,
        "expert_of": np.broadcast_to(np.arange(E, dtype=np.float32)[None, :, None], (P, E, NT)).copy(),
        "keep": np.broadcast_to((np.arange(E * NT) % NT != 0).astype(np.float32), (P, E * NT)).copy(),
        "block_no": np.broadcast_to(np.arange(NBLK_LOADED, dtype=np.float32)[None, :, None], (1, NBLK_LOADED, E)).copy(),
        "dest_c": dest,
        "xg_init": xg,
    }


def kernel(x, txt, L0_tok_W0, L0_tok_b0, L0_tok_W1, L0_tok_b1, L0_tok_W2, L0_tok_b2, L0_tok_Wf, L0_tok_bf,
           L0_tok_idx0, L0_tok_idx1, L0_tok_idx2, L0_attn_w_qkv, L0_attn_w_o, L0_ffn_Wr, L0_ffn_Wi, L0_ffn_bi,
           L0_ffn_Wo, L0_ffn_bo):
    import concourse.bacc as bacc
    from concourse.bass_utils import run_bass_kernel_spmd

    x = np.asarray(x)

    def patches(p):
        n = IMG // p
        return x.reshape(B, CH, n, p, n, p).transpose(2, 4, 0, 3, 5, 1)

    def halves(w):
        return w.reshape(2, KH, -1).transpose(1, 0, 2)

    a = np.asarray
    arrays = {
        "xp0": patches(1).reshape(4096, B * 3),
        "xp1": patches(2).reshape(1024, B * 12),
        "xp2": patches(4).transpose(2, 0, 1, 3, 4, 5).reshape(B * 256, 48),
        "txt": a(txt),
        "W0T": a(L0_tok_W0).T, "b0": a(L0_tok_b0).reshape(-1, 1),
        "W1T": a(L0_tok_W1).T.reshape(2, 96, EMB).transpose(1, 0, 2), "b1": a(L0_tok_b1).reshape(-1, 1),
        "W2T": a(L0_tok_W2).T.reshape(8, 96, EMB).transpose(1, 0, 2), "b2": a(L0_tok_b2).reshape(-1, 1),
        "WfT": a(L0_tok_Wf).T, "bf": a(L0_tok_bf).reshape(1, -1),
        "idx0": a(L0_tok_idx0), "idx1": a(L0_tok_idx1), "idx2": a(L0_tok_idx2),
        "wqkv": halves(a(L0_attn_w_qkv).transpose(2, 1, 0, 3).reshape(D, 3 * DI)),
        "wo": a(L0_attn_w_o).reshape(NPAIR, P, D).transpose(1, 0, 2),
        "WrT": halves(a(L0_ffn_Wr).T),
        "WiT": halves(a(L0_ffn_Wi).transpose(2, 0, 1).reshape(D, E * F)),
        "bi": a(L0_ffn_bi).reshape(1, -1),
        "WoT": a(L0_ffn_Wo).transpose(0, 2, 1).reshape(E * FT, P, D).transpose(1, 0, 2),
        "bo": a(L0_ffn_bo).reshape(1, -1),
    }
    arrays.update(shape_constants())
    nc = bacc.Bacc("TRN2", target_bir_lowering=False, num_devices=1)
    given, aps = {}, {}
    for name, value in arrays.items():
        value = np.ascontiguousarray(value)
        given["in_" + name] = value
        aps[name] = nc.dram_tensor("in_" + name, value.shape, mybir.dt.from_np(value.dtype), kind="ExternalInput").ap()
    aps["xg"] = nc.dram_tensor("routed_rows", (NBLK_LOADED * P, ROW), F32, kind="Internal").ap()
    aps["z"] = nc.dram_tensor("routed_results", (2 * NTOK + NBLK_LOADED * P, D), F32, kind="Internal").ap()
    aps["out"] = nc.dram_tensor("out_0", (B, SEQ, D), F32, kind="ExternalOutput").ap()
    fused_layer_kernel(nc, **aps)
    result = run_bass_kernel_spmd(nc, [given], core_ids=[0])
    return result.results[0]["out_0"]
```

```python
from contextlib import ExitStack

import numpy as np
import concourse.bass as bass
from concourse import mybir

F32 = mybir.dt.float32
F32R = mybir.dt.float32r
I32 = mybir.dt.int32
U32 = mybir.dt.uint32
ALU = mybir.AluOpType
ACT = mybir.ActivationFunctionType
AX_X = mybir.AxisListType.X

P = 128
B = 8
IMG, CH, GP = 64, 3, 16
TOK_IMG = IMG * IMG // GP
TOK_TXT = 128
SEQ = TOK_IMG + TOK_TXT
D = 192
KH = D // 2
MT = SEQ // P
NT = B * MT
NTOK = NT * P
HEADS, DH = 12, 64
NPAIR = HEADS // 2
DI = HEADS * DH
EMB = 64
E = 8
F = 768
FT = F // P
FH = F // 2
NBLK = 2 * NT + E
NBLK_LOADED = NBLK + 4
ROW = D + 2
EPS = 1e-5
PRIMED = 1


class FillCount:

    def __init__(self, engine, free, ahead, per_batch):
        self.engine, self.free, self.n = engine, free, [0, 0]
        self.ahead, self.per_batch, self.in_loop = ahead, per_batch, False

    def enter_loop(self):
        assert self.n == list(self.ahead)
        self.in_loop, self.n = True, [0, 0]

    def leave_loop(self):
        assert self.n == list(self.per_batch)

    def done(self, j, b):
        if not self.in_loop:
            return self.n[j]
        return b * self.per_batch[j] + self.ahead[j] + self.n[j]

    def next(self, j, b):
        self.engine.wait_ge(self.free[j], self.done(j, b) + PRIMED)
        self.n[j] += 1
        return j

    def settled(self, b, but=(0, 0)):
        for j in range(2):
            self.engine.wait_ge(self.free[j], self.done(j, b) - but[j] + PRIMED)


FILLS = ((6, 6), (12, 11))
SPLIT_FILLS = ((3, 3), (7, 7))


def fused_layer_kernel(nc, xp0, xp1, xp2, txt, W0T, b0, W1T, b1, W2T, b2, WfT, bf, idx0, idx1, idx2,
                       wqkv, wo, WrT, WiT, bi, WoT, bo, base2, ident_c, tri_c, A1, A2, expert_of, keep,
                       block_no, dest_c, xg_init, xg, z, out):
    ctx = ExitStack()

    def sb(stack, name, shape, dt=F32):
        return stack.enter_context(nc.sbuf_tensor(name, shape, dt))

    def sem(name):
        return ctx.enter_context(nc.semaphore(name))

    with ctx:
        h = sb(ctx, "h", [P, NT + MT, D])
        wi = sb(ctx, "wi", [KH + 1, 2, E * F])
        wo2 = sb(ctx, "wo2", [P, E * FT, D])
        ident = sb(ctx, "ident", [P, P])
        tri = sb(ctx, "tri", [P, P])
        ones = sb(ctx, "ones", [P, P])
        wr = sb(ctx, "wr", [KH, 2, E])
        epsc = sb(ctx, "epsc", [P, 1])
        stats = sb(ctx, "stats", [P, NT + MT, 6])
        mv = sb(ctx, "mv", [P, NT + MT, 2])
        rstd = sb(ctx, "rstd", [P, NT + MT])

        tk = ExitStack()
        i0 = sb(tk, "i0", [P, 2, GP], I32)
        i1 = sb(tk, "i1", [64, GP], I32)
        i2 = sb(tk, "i2", [P, GP], I32)
        i2b = sb(tk, "i2b", [P, GP], I32)
        g0 = sb(tk, "g0", [P, 2, GP, B * 3])
        g1 = sb(tk, "g1", [64, GP, B * 12])
        g2 = sb(tk, "g2", [P, GP, 48])
        g0b = sb(tk, "g0b", [P, 2, B, GP * 3])
        g1b = sb(tk, "g1b", [64, B, GP * 12])
        g0t = sb(tk, "g0t", [48, B * TOK_IMG])
        g1t = sb(tk, "g1t", [96, 2, 512])
        g2t = sb(tk, "g2t", [96, 8, P])
        e1 = sb(tk, "e1", [64, 512])
        e2 = sb(tk, "e2", [P, EMB])
        ya = sb(tk, "ya", [P, B * TOK_IMG])
        yb = sb(tk, "yb", [EMB, B * TOK_IMG])
        a1 = sb(tk, "a1", [64, TOK_IMG])
        a2 = sb(tk, "a2", [P, B, TOK_IMG])
        w0 = sb(tk, "w0", [48, EMB])
        w1 = sb(tk, "w1", [96, 2, EMB])
        w2 = sb(tk, "w2", [96, 8, EMB])
        wfa = sb(tk, "wfa", [P, D])
        wfb = sb(tk, "wfb", [EMB, D])
        bca = sb(tk, "bca", [P, 1])
        bcb = sb(tk, "bcb", [EMB, 1])
        bf_bc = sb(tk, "bf_bc", [P, D])
        tk.close()

        at = ExitStack()
        wq = [sb(at, f"wq{s}", [KH, 2, 3 * DI], F32R) for s in range(2)]
        wot = sb(at, "wot", [P, NPAIR, D])
        xnb = sb(at, "xnb", [P, MT, D])
        xb = [sb(at, f"xb{s}", [KH, 2, SEQ], F32R) for s in range(2)]
        v = sb(at, "v", [P, MT, DI])
        qT = [[sb(at, f"qT{i}{s}", [P, SEQ], F32R) for s in range(2)] for i in range(2)]
        kz = [[[sb(at, f"kz{i}{j}{s}", [P, SEQ], F32R) for s in range(2)] for j in range(2)] for i in range(2)]
        pr = [sb(at, f"pr{i}", [P, MT, SEQ]) for i in range(2)]
        pT = sb(at, "pT", [P, MT, SEQ])
        nmax = sb(at, "nmax", [P, 2, MT])
        rsum = sb(at, "rsum", [P, 2, MT])
        rinv = sb(at, "rinv", [P, 2, MT])
        oT = sb(at, "oT", [P, NPAIR, SEQ])
        at.close()

        mo = ExitStack()
        bo_bc = sb(mo, "bo_bc", [P, E * D])
        xn = [sb(mo, f"xn{c}", [P, NT, ROW]) for c in range(2)]
        st = sb(mo, "st", [P, 4, D])
        xt = sb(mo, "xt", [KH, 2, 4 * P])
        logits = sb(mo, "logits", [P, NT, E])
        mx8 = sb(mo, "mx8", [P, NT, 8])
        ix8 = sb(mo, "ix8", [P, NT, 8], U32)
        ixf = sb(mo, "ixf", [P, 2, NT])
        eo = sb(mo, "eo", [P, E, NT])
        kp = sb(mo, "kp", [P, E * NT])
        bn = sb(mo, "bn", [1, NBLK_LOADED, E])
        m01 = sb(mo, "m01", [P, 2, E, NT])
        msum = sb(mo, "msum", [P, E * NT])
        tot = sb(mo, "tot", [P, E * NT])
        inc = sb(mo, "inc", [P, E * NT])
        nbi = sb(mo, "nbi", [P, E], I32)
        nbf = sb(mo, "nbf", [P, E])
        binc = sb(mo, "binc", [P, E])
        base = sb(mo, "base", [P, E])
        slotf = sb(mo, "slotf", [P, 2, NT])
        sloti = sb(mo, "sloti", [P, 2, NT], I32)
        wts = sb(mo, "wts", [P, 2, NT])
        tmp = sb(mo, "tmp", [P, E * NT])
        bcmp = sb(mo, "bcmp", [1, NBLK_LOADED, E])
        bexf = sb(mo, "bexf", [1, NBLK_LOADED])
        bex = sb(mo, "bex", [1, NBLK_LOADED], I32)
        xr = [sb(mo, f"xr{u}", [P, ROW]) for u in range(2)]
        dst = [sb(mo, f"dst{u}", [P, 2]) for u in range(2)]
        dst_next = [sb(mo, f"dst_next{u}", [P, 2]) for u in range(2)]
        dest = sb(mo, "dest", [P, 2, NT], I32)
        xT = [sb(mo, f"xT{u}", [KH + 1, 2, P]) for u in range(2)]
        hs = sb(mo, "hs", [P, F])
        hT = sb(mo, "hT", [P, FT, P])
        yv = [sb(mo, f"yv{u}", [P, D]) for u in range(2)]
        zc = [[sb(mo, f"z{c}{u}", [P, MT, D]) for u in range(2)] for c in range(2)]
        mo.close()

        bank = [ctx.enter_context(nc.psum_tensor(f"bank{i}", [P, 512], F32)) for i in range(8)]

        s_idx, s_const, s_g, s_i2, s_tokw, s_txt, s_moew = map(sem, (
            "indices_loaded", "constants_loaded", "patches_gathered", "level2_index_ready",
            "tokenizer_weights_loaded", "text_loaded", "expert_weights_loaded"))
        s_attw, s_xginit = sem("attention_weights_loaded"), sem("slots_initialised")
        s_setup = sem("constants_set")
        t_grp = sem("patches_regrouped")
        t_pe, t_ev, t_h = sem("tokenizer_product_ready"), sem("tokenizer_product_copied"), sem("image_tokens_ready")
        ln_chain, ln_var, ln_std, ln_rstd = sem("ln_dve_step"), sem("variances_ready"), sem("std_ready"), sem("rstd_ready")
        a_xn = sem("batch_normalised")
        x_full = [sem("projection0_ready"), sem("projection1_ready")]
        x_hi = [sem("projection0_high_part_ready"), sem("projection1_high_part_ready")]
        w_split, w_high = sem("attention_weights_split"), sem("attention_weights_high_parts")
        x_free = [sem("projection0_copied"), sem("projection1_copied")]
        s_full, s_max, exp_done = sem("scores_ready"), sem("max_ready"), [sem(f"exp_done{m}") for m in range(MT)]
        r_ready, p_ready, p_free = sem("sum_inverted"), sem("probs_ready"), [sem("probs0_used"), sem("probs1_used")]
        t_full, t_free = sem("probs_transposed"), [sem("transpose0_copied"), sem("transpose1_copied")]
        o_full, o_free = sem("head_pair_ready"), sem("head_pair_copied")
        h_done = sem("attention_added")
        r_ln, r_copy, r_T, r_Tev, r_log, r_logev = map(sem, (
            "router_input_ready", "routed_rows_copied", "router_input_transposed", "router_transpose_copied",
            "logits_ready", "logits_copied"))
        r_chain, r_d, r_e, r_m, r_cnt, r_slot, r_blk = map(sem, (
            "router_dve_step", "logit_gap_ready", "gap_exp_ready", "choice_masks_ready", "ranks_ready", "slots_ready",
            "block_experts_ready"))
        s_scat = sem("rows_scattered")
        b_load = [sem("block_loaded0"), sem("block_loaded1")]
        b_x, b_xev, b_h, b_g, b_t, b_tev, b_y, b_yev, b_yw = map(sem, (
            "block_transposed", "block_transpose_copied", "hidden_ready", "gelu_done", "hidden_transposed",
            "hidden_transpose_copied", "expert_out_ready", "expert_bias_added", "expert_out_weighted"))
        b_addr, b_dst = sem("next_addresses_copied"), sem("addresses_ready")
        y_free = [sem("result0_free"), sem("result1_free")]
        b_scat = [sem("result_scattered0"), sem("result_scattered1")]
        z_load = [sem("results_loaded0"), sem("results_loaded1")]
        z_chain, z_sum, z_out = sem("first_result_added"), sem("output_tile_ready"), sem("output_stored")

        primed = [*x_free, *exp_done, *p_free, *t_free, o_free, r_T, r_Tev, r_logev, r_copy, b_xev, b_tev, b_yev, *y_free]

        block = ctx.enter_context(nc.Block())
        h_flat = h[:].rearrange("p t d -> p (t d)")

        def staged(kt, part):
            if kt == 0:
                return oT[0:KH, 2 * part:2 * part + 2, :].rearrange("p a b -> p (a b)")
            return v[0:KH, part, :]

        @block.sync
        def _(sp):
            sp.dma_start(i0[:], idx0.rearrange("(a t i) -> t a i", a=2, i=GP)).then_inc(s_idx, 16)
            sp.dma_start(i1[:], idx1.rearrange("(t i) -> t i", i=GP)).then_inc(s_idx, 16)
            for b in range(B):
                sp.dma_start(i2[16 * b:16 * b + 16, :], idx2.rearrange("(t i) -> t i", i=GP)).then_inc(s_idx, 16)
            sp.dma_start(i2b[:], base2).then_inc(s_idx, 16)
            for dst_, src in ((ident, ident_c), (tri, tri_c), (wr, WrT)):
                sp.dma_start(dst_[:], src).then_inc(s_const, 16)
            for dst_, src in ((w0, W0T), (w1, W1T), (w2, W2T), (a1, A1), (a2, A2)):
                sp.dma_start(dst_[:], src).then_inc(s_tokw, 16)
            sp.dma_start(wfa[:], WfT[0:P, :]).then_inc(s_tokw, 16)
            sp.dma_start(wfb[:], WfT[P:D, :]).then_inc(s_tokw, 16)
            sp.dma_start(bca[0:EMB, :], b0).then_inc(s_tokw, 16)
            sp.dma_start(bca[EMB:P, :], b1).then_inc(s_tokw, 16)
            sp.dma_start(bcb[:], b2).then_inc(s_tokw, 16)
            sp.dma_start(bf_bc[:], bf.broadcast_to([P, D])).then_inc(s_tokw, 16)
            for b in range(B):
                sp.dma_start(h[:, b * MT + 2, :], txt[b]).then_inc(s_txt, 16)
            sp.dma_start(wi[0:KH, :, :], WiT).then_inc(s_moew, 16)
            sp.dma_start(wi[KH:KH + 1, 1, :], bi).then_inc(s_moew, 16)
            sp.dma_start(wo2[:], WoT).then_inc(s_moew, 16)
            sp.dma_start(xg, xg_init).then_inc(s_xginit, 16)
            sp.wait_ge(t_h, 16)
            for kt in range(2):
                for part in range(3):
                    sp.dma_start(staged(kt, part), wqkv[:, kt, part * DI:(part + 1) * DI]).then_inc(s_attw, 16)
            sp.dma_start(wot[:], wo).then_inc(s_attw, 16)
            sp.wait_ge(h_done, B * MT)
            sp.dma_start(bo_bc[:], bo.broadcast_to([P, E * D])).then_inc(s_moew, 16)
            sp.dma_start(eo[:], expert_of).then_inc(s_attw, 16)
            sp.dma_start(kp[:], keep).then_inc(s_attw, 16)
            sp.dma_start(bn[:], block_no).then_inc(s_attw, 16)
            sp.dma_start(dest[:], dest_c).then_inc(s_attw, 16)
            sp.wait_ge(s_scat, 16 * 2 * NT)
            for u in range(2):
                sp.dma_start(xr[u][:], xg[u * P:(u + 1) * P, :]).then_inc(b_load[u], 16)
            with sp.Fori(0, NBLK // 2) as i:
                for u in range(2):
                    sp.wait_ge(b_x, 2 * i + u + 1)
                    sp.wait_ge(b_addr, 2 * i + u + 1)
                    sp.dma_start(xr[u][:], xg[bass.ds((2 * i + 2 + u) * P, P), :]).then_inc(b_load[u], 16)
            for u in range(2):
                sp.wait_ge(b_scat[u], 16 * (NBLK // 2))
                sp.wait_ge(b_load[u], 16 * (NBLK // 2 + 1))
            sp.wait_ge(b_x, NBLK + 2)
            for b in range(B):
                if b >= 2:
                    sp.wait_ge(z_sum, b - 1)
                    sp.wait_ge(z_out, 16 * (b - 1))
                for c in range(2):
                    src = z[c * NTOK + b * SEQ:c * NTOK + (b + 1) * SEQ, :].rearrange("(m p) d -> p m d", p=P)
                    sp.dma_start(zc[c][b % 2][:], src).then_inc(z_load[b % 2], 16)
                if b >= 1:
                    sp.wait_ge(z_sum, b)
                    sp.dma_start(out[b - 1].rearrange("(m p) d -> p m d", p=P), h[:, (b - 1) * MT:b * MT, :]).then_inc(z_out, 16)
            sp.wait_ge(z_sum, B)
            sp.dma_start(out[B - 1].rearrange("(m p) d -> p m d", p=P), h[:, (B - 1) * MT:B * MT, :]).then_inc(z_out, 16)
            sp.wait_ge(z_out, 16 * B)

        @block.gpsimd
        def _(pool):
            for s in primed:
                pool.sem_inc(s, PRIMED)
            pool.memset(ones[:], 1.0).then_inc(s_setup, 1)
            pool.memset(epsc[:], EPS).then_inc(s_setup, 1)
            pool.memset(h[:, NT:NT + MT, :], 0.0).then_inc(s_setup, 1)
            pool.wait_ge(s_idx, 16 * (B + 3))
            pool.tensor_tensor(i2[:], i2[:], i2b[:], ALU.add).then_inc(s_i2, 1)
            for i in range(GP):
                for a in range(2):
                    pool.indirect_dma_start(out=g0[:, a, i, :], out_offset=None, in_=xp0,
                                            in_offset=bass.IndirectOffsetOnAxis(ap=i0[:, a, i:i + 1], axis=0)).then_inc(s_g, 16)
                pool.indirect_dma_start(out=g1[:, i, :], out_offset=None, in_=xp1,
                                        in_offset=bass.IndirectOffsetOnAxis(ap=i1[:, i:i + 1], axis=0)).then_inc(s_g, 16)
            pool.wait_ge(s_i2, 1)
            for i in range(GP):
                pool.indirect_dma_start(out=g2[:, i, :], out_offset=None, in_=xp2,
                                        in_offset=bass.IndirectOffsetOnAxis(ap=i2[:, i:i + 1], axis=0)).then_inc(s_g, 16)
            pool.wait_ge(t_h, 16)
            for i in range(2):
                for s in range(2):
                    pool.memset(kz[i][0][s][DH:P, :].bitcast(F32), 0.0).then_inc(s_setup, 1)
                    pool.memset(kz[i][1][s][0:DH, :].bitcast(F32), 0.0).then_inc(s_setup, 1)
            pool.wait_ge(h_done, B * MT)
            for u in range(2):
                pool.memset(xT[u][KH:KH + 1, 1, :], 1.0).then_inc(s_setup, 1)
            pool.wait_ge(s_xginit, 16)
            pool.wait_ge(r_slot, 1)
            pool.wait_ge(r_ln, 6)
            pool.wait_ge(r_copy, 6 + PRIMED)
            for c in range(2):
                for t in range(NT):
                    pool.indirect_dma_start(out=xg, out_offset=bass.IndirectOffsetOnAxis(ap=sloti[:, c, t:t + 1], axis=0),
                                            in_=xn[c][:, t, :], in_offset=None).then_inc(s_scat, 16)
            with pool.Fori(0, NBLK // 2) as i:
                for u in range(2):
                    pool.wait_ge(b_yw, 2 * i + u + 1)
                    pool.nop(nofuse=True)
                    pool.indirect_dma_start(out=z, out_offset=bass.IndirectOffsetOnAxis(ap=dst[u][:, 0:1].bitcast(I32), axis=0),
                                            in_=yv[u][:], in_offset=None).then_inc(b_scat[u], 16)
                    pool.wait_ge(b_scat[u], 16 * (i + 1))
                    pool.sem_inc(y_free[u], 1)

        @block.tensor
        def _(pe):
            pe.wait_ge(s_const, 48)
            pe.wait_ge(s_g, 16 * 4 * GP)
            pe.wait_ge(t_grp, 3)
            k = 0

            def start_product(first):
                if first >= 4:
                    pe.wait_ge(t_ev, first - 3)
            for b in range(0, B, 2):
                start_product(k)
                for j in range(4):
                    last = pe.transpose(bank[k % 4][0:48, j * P:(j + 1) * P],
                                        g0b[:, j % 2, b + j // 2, :], ident[:])
                last.then_inc(t_pe, 1)
                k += 1
            for kt in range(2):
                start_product(k)
                for b in range(B):
                    last = pe.transpose(bank[k % 4][0:96, b * 64:(b + 1) * 64],
                                        g1b[:, b, kt * 96:(kt + 1) * 96], ident[0:64, 0:64])
                last.then_inc(t_pe, 1)
                k += 1
            for kt in range(2):
                start_product(k)
                for j in range(4):
                    last = pe.transpose(bank[k % 4][0:96, j * P:(j + 1) * P],
                                        g2[:, (kt * 4 + j) * 2:(kt * 4 + j) * 2 + 2, :].rearrange("p i c -> p (i c)"), ident[:])
                last.then_inc(t_pe, 1)
                k += 1
            pe.wait_ge(s_tokw, 16 * 11)
            pe.wait_ge(t_ev, 6)
            for b in range(B):
                for kt in range(2):
                    last = pe.matmul(bank[k % 4][0:64, b * 64:(b + 1) * 64], g1t[:, kt, b * 64:(b + 1) * 64], w1[:, kt, :],
                                     start=kt == 0, stop=kt == 1)
            last.then_inc(t_pe, 1)
            k += 1
            pe.wait_ge(t_ev, 8)
            for kt in range(8):
                last = pe.matmul(bank[k % 4][:, 0:EMB], g2t[:, kt, :], w2[:, kt, :], start=kt == 0, stop=kt == 7)
            last.then_inc(t_pe, 1)
            k += 1
            for b in range(0, B, 2):
                start_product(k)
                pe.matmul(bank[k % 4][0:EMB, :], w0[:], g0t[:, b * TOK_IMG:(b + 2) * TOK_IMG],
                          start=True, stop=True).then_inc(t_pe, 1)
                k += 1
            for b in range(0, B, 2):
                start_product(k)
                for j in range(2):
                    last = pe.matmul(bank[k % 4][EMB:P, j * TOK_IMG:(j + 1) * TOK_IMG],
                                     e1[:, (b + j) * 64:(b + j + 1) * 64], a1[:], start=True, stop=True)
                last.then_inc(t_pe, 1)
                k += 1
            for b in range(0, B, 2):
                start_product(k)
                for j in range(2):
                    last = pe.matmul(bank[k % 4][0:EMB, j * TOK_IMG:(j + 1) * TOK_IMG],
                                     e2[:], a2[:, b + j, :], start=True, stop=True)
                last.then_inc(t_pe, 1)
                k += 1
            pe.wait_ge(t_ev, 22)
            for b in range(B):
                for a in range(2):
                    start_product(k)
                    c0 = b * TOK_IMG + a * P
                    pe.matmul(bank[k % 4][:, 0:D], ya[:, c0:c0 + P], wfa[:], start=True, stop=False)
                    pe.matmul(bank[k % 4][:, 0:D], yb[:, c0:c0 + P], wfb[:], start=False, stop=True).then_inc(t_pe, 1)
                    k += 1

            PB = [bank[0], bank[1]]
            SB = bank[2:5]
            TB = bank[5:7]
            OB = bank[7]
            pe.wait_ge(s_attw, 16 * 7)
            pe.wait_ge(w_split, 6)
            pe.wait_ge(s_setup, 11)
            PARTS = ((0, 0), (0, 1), (1, 0))
            fills = FillCount(pe, x_free, *FILLS)

            def split_product(o, lhsT, rhs, kts):
                steps_ = [(kt, a, c) for kt in range(kts) for a, c in PARTS]
                for i, (kt, a, c) in enumerate(steps_):
                    last = pe.matmul(o, lhsT(kt, a), rhs(kt, c), start=i == 0, stop=i == len(steps_) - 1)
                return last

            def transpose_tokens(b, nth):
                pe.wait_ge(a_xn, nth + 1)
                for kt in range(2):
                    o = PB[fills.next(kt, b)]
                    for m in range(MT):
                        last = pe.transpose(o[0:KH, m * P:(m + 1) * P], xnb[:, m, kt * KH:(kt + 1) * KH], ident[:])
                    last.then_inc(x_full[kt], 1)

            def values(b, m, j):
                o = PB[fills.next(j, b)]
                c0 = 2 * DI + j * 384
                split_product(o[:, 0:384], lambda kt, a: xb[a][:, kt, m * P:(m + 1) * P],
                              lambda kt, c: wq[c][:, kt, c0:c0 + 384], 2).then_inc(x_full[j], 1)

            def project(b, p, j):
                o = PB[fills.next(j, b)]
                c0 = j * DI + p * P
                split_product(o[:, 0:SEQ], lambda kt, a: wq[a][:, kt, c0:c0 + P],
                              lambda kt, c: xb[c][:, kt, :], 2).then_inc(x_full[j], 1)

            def score(b, n, m):
                p = n // 2
                pe.wait_ge(exp_done[m], b * HEADS + n + PRIMED)
                split_product(SB[m][:, 0:SEQ], lambda kt, a: qT[p % 2][a][:, m * P:(m + 1) * P],
                              lambda kt, c: kz[p % 2][n % 2][c][:], 1).then_inc(s_full, 1)

            def transpose_probs(b, n, j):
                e = n * MT + j
                pe.wait_ge(t_free[e % 2], b * (HEADS * MT // 2) + e // 2 + PRIMED)
                for m in range(MT):
                    last = pe.transpose(TB[e % 2][:, m * P:(m + 1) * P], pr[n % 2][:, m, j * P:(j + 1) * P], ident[:])
                last.then_inc(t_full, 1)

            def fill(b, n):
                if n <= 7:
                    project(b, n // 2 + 2, n % 2)
                elif n == 8:
                    transpose_tokens(b, b + 1)
                elif n == 9:
                    fills.settled(b)
                    project(b, 0, 0)
                    project(b, 0, 1)
                elif n == 10:
                    project(b, 1, 0)

            transpose_tokens(0, 0)
            fills.settled(0)
            for m in range(MT):
                for j in range(2):
                    values(0, m, j)
            project(0, 0, 0)
            project(0, 0, 1)
            project(0, 1, 0)
            project(0, 1, 1)
            fills.settled(0)
            for m in range(MT):
                score(0, 0, m)
            fills.enter_loop()
            with pe.Fori(0, B) as b:
                for n in range(HEADS):
                    p = n // 2
                    if n % 2 == 1:
                        fills.settled(b, (1, 1 if n == 9 else 0))
                    for m in range(MT):
                        score(b, n + 1, m)
                    pe.wait_ge(p_ready, b * HEADS + n + 1)
                    transpose_probs(b, n, 0)
                    transpose_probs(b, n, 1)
                    fill(b, n)
                    transpose_probs(b, n, 2)
                    if n % 2 == 0:
                        pe.wait_ge(o_free, b * NPAIR + p + PRIMED)
                    for j in range(MT):
                        e = n * MT + j
                        pe.wait_ge(t_free[e % 2], b * (HEADS * MT // 2) + e // 2 + 1 + PRIMED)
                        last = pe.matmul(OB[(n % 2) * DH:(n % 2) * DH + DH, 0:SEQ], v[:, j, n * DH:(n + 1) * DH],
                                         pT[:, j, :], start=j == 0, stop=j == MT - 1)
                        if j == 0:
                            last.then_inc(p_free[n % 2], 1)
                    if n % 2 == 1:
                        last.then_inc(o_full, 1)
                for m in range(MT):
                    for j in range(2):
                        values(b, m, j)
                pe.wait_ge(o_free, b * NPAIR + NPAIR + PRIMED)
                for m in range(MT):
                    o = PB[fills.next(m % 2, b)]
                    for p in range(NPAIR):
                        last = pe.matmul(o[:, 0:D], oT[:, p, m * P:(m + 1) * P], wot[:, p, :], start=p == 0, stop=p == NPAIR - 1)
                    last.then_inc(x_full[m % 2], 1)
                project(b, 1, 1)
                fills.leave_loop()

            pe.wait_ge(h_done, B * MT)
            with pe.Fori(0, NT // 4) as g:
                pe.wait_ge(r_ln, g + 1)
                pe.wait_ge(r_Tev, 2 * g + PRIMED)
                for kt in range(2):
                    for j in range(4):
                        last = pe.transpose(bank[kt][0:KH, j * P:(j + 1) * P], st[:, j, kt * KH:(kt + 1) * KH], ident[:])
                    last.then_inc(r_T, 1)
                pe.wait_ge(r_Tev, 2 * g + 2 + PRIMED)
                pe.wait_ge(r_logev, g + PRIMED)
                for j in range(4):
                    for kt in range(2):
                        last = pe.matmul(bank[2][:, j * E:(j + 1) * E], xt[:, kt, j * P:(j + 1) * P], wr[:, kt, :],
                                         start=kt == 0, stop=kt == 1)
                last.then_inc(r_log, 1)
            pe.wait_ge(r_m, 1)
            pe.matmul(bank[0][:, 0:E * NT], tri[:], msum[:], start=True, stop=True)
            pe.matmul(bank[1][:, 0:E * NT], ones[:], msum[:], start=True, stop=True).then_inc(r_cnt, 1)

            HB, TT, YB, XB = bank[0:2], bank[2:4], bank[4:6], bank[6]

            def block_transpose(n, u):
                pe.wait_ge(b_load[u], 16 * ((n - u) // 2 + 1) if isinstance(n, int) else 8 * (n - u) + 16)
                pe.wait_ge(b_xev, n + PRIMED)
                for kt in range(2):
                    last = pe.transpose(XB[0:KH, kt * P:(kt + 1) * P], xr[u][:, kt * KH:(kt + 1) * KH], ident[:])
                last.then_inc(b_x, 1)

            def hidden(n, u, expert):
                pe.wait_ge(b_xev, n + 1 + PRIMED)
                for f in range(2):
                    cols = bass.ds(expert * F + f * FH, FH)
                    pe.matmul(HB[f][:, 0:FH], xT[u][0:KH, 0, :], wi[0:KH, 0, cols], start=True, stop=False)
                    pe.matmul(HB[f][:, 0:FH], xT[u][:, 1, :], wi[:, 1, cols], start=False, stop=True).then_inc(b_h, 1)

            def expert_of_block(n):
                return pe.value_load(bex[0:1, bass.ds(n, 1)], min_val=0, max_val=E - 1)

            pe.wait_ge(s_moew, 64)
            pe.wait_ge(s_setup, 13)
            pe.wait_ge(r_blk, 1)
            block_transpose(0, 0)
            block_transpose(1, 1)
            hidden(0, 0, expert_of_block(0))
            with pe.Fori(0, NBLK // 2) as i:
                ex = [expert_of_block(2 * i + u) for u in range(3)]
                for u in range(2):
                    n = 2 * i + u
                    for f in range(2):
                        pe.wait_ge(b_g, 2 * n + f + 1)
                        pe.wait_ge(b_tev, 2 * n + PRIMED)
                        for j in range(3):
                            last = pe.transpose(TT[f][:, j * P:(j + 1) * P], hs[:, (3 * f + j) * P:(3 * f + j + 1) * P], ident[:])
                        last.then_inc(b_t, 1)
                    block_transpose(n + 2, u)
                    hidden(n + 1, 1 - u, ex[u + 1])
                    pe.wait_ge(b_yev, n + PRIMED)
                    for j in range(FT):
                        if j % 3 == 0:
                            pe.wait_ge(b_tev, 2 * n + j // 3 + 1 + PRIMED)
                        last = pe.matmul(YB[u][:, 0:D], hT[:, j, :], wo2[:, bass.ds(ex[u] * FT + j, 1), :].rearrange("p o d -> p (o d)"),
                                         start=j == 0, stop=j == FT - 1)
                    last.then_inc(b_y, 1)

        @block.scalar
        def _(act):
            def tok_copy(k, out_, in_, bias=None):
                act.wait_ge(t_pe, k + 1)
                act.wait_ge(t_ev, k)
                if bias is None:
                    act.activation(out_, in_, ACT.Copy).then_inc(t_ev, 1)
                else:
                    act.activation(out_, in_, ACT.Identity, bias=bias).then_inc(t_ev, 1)

            act.wait_ge(s_tokw, 16 * 11)
            k = 0
            for j in range(4):
                tok_copy(k, g0t[:, j * 512:(j + 1) * 512], bank[k % 4][0:48, :])
                k += 1
            for kt in range(2):
                tok_copy(k, g1t[:, kt, :], bank[k % 4][0:96, :])
                k += 1
            for kt in range(2):
                tok_copy(k, g2t[:, kt * 4:(kt + 1) * 4, :].rearrange("p a b -> p (a b)"), bank[k % 4][0:96, :])
                k += 1
            tok_copy(k, e1[:], bank[k % 4][0:64, :])
            k += 1
            tok_copy(k, e2[:], bank[k % 4][:, 0:EMB])
            k += 1
            for j in range(4):
                tok_copy(k, ya[0:EMB, j * 512:(j + 1) * 512], bank[k % 4][0:EMB, :], bca[0:EMB, :])
                k += 1
            for j in range(4):
                tok_copy(k, ya[EMB:P, j * 512:(j + 1) * 512], bank[k % 4][EMB:P, :], bca[EMB:P, :])
                k += 1
            for j in range(4):
                tok_copy(k, yb[:, j * 512:(j + 1) * 512], bank[k % 4][0:EMB, :], bcb[:])
                k += 1
            act.wait_ge(s_setup, 2)
            act.wait_ge(ln_var, 1)
            act.activation(rstd[:], mv[:, :, 1], ACT.Sqrt, bias=epsc[:]).then_inc(ln_std, 1)

            for kt in range(2):
                for part in range(3):
                    if kt == part == 0:
                        act.wait_ge(s_attw, 16 * 7)
                    act.activation(wq[0][:, kt, part * DI:(part + 1) * DI], staged(kt, part), ACT.Copy).then_inc(w_high, 1)
            seen = FillCount(act, None, *FILLS)

            def full(j, b):
                act.wait_ge(x_full[j], seen.done(j, b) + 1)
                seen.n[j] += 1

            def tokens(b):
                for kt in range(2):
                    full(kt, b)
                    act.activation(xb[0][:, kt, :], bank[kt][0:KH, 0:SEQ], ACT.Copy).then_inc(x_hi[kt], 1)

            def values(b, m, j):
                if j == 0:
                    full(0, b)
                    act.activation(v[:, m, 0:384], bank[0][:, 0:384], ACT.Copy).then_inc(x_free[0], 1)
                else:
                    seen.n[1] += 1

            def projected(b, p, j):
                full(j, b)
                if j == 0:
                    act.activation(qT[p % 2][0][:], bank[0][:, 0:SEQ], ACT.Copy, scale=DH ** -0.5).then_inc(x_hi[0], 1)
                else:
                    act.activation(kz[p % 2][0][0][0:DH, :], bank[1][0:DH, 0:SEQ], ACT.Copy)
                    act.activation(kz[p % 2][1][0][DH:P, :], bank[1][DH:P, 0:SEQ], ACT.Copy).then_inc(x_hi[1], 1)

            def fill_copied(b, n):
                if n <= 7:
                    projected(b, n // 2 + 2, n % 2)
                elif n == 8:
                    tokens(b)
                elif n == 9:
                    projected(b, 0, 0)
                    projected(b, 0, 1)
                elif n == 10:
                    projected(b, 1, 0)

            def exp(b, n, m):
                act.wait_ge(s_max, b * HEADS * MT + n * MT + m + 1)
                act.activation(pr[n % 2][:, m, :], bank[2 + m][:, 0:SEQ], ACT.Exp, bias=nmax[:, n % 2, m:m + 1],
                               accum_out=rsum[:, n % 2, m:m + 1]).then_inc(exp_done[m], 1)

            tokens(0)
            act.wait_ge(w_split, 6)
            for m in range(MT):
                for j in range(2):
                    values(0, m, j)
            projected(0, 0, 0)
            projected(0, 0, 1)
            projected(0, 1, 0)
            projected(0, 1, 1)
            for m in range(MT):
                exp(0, 0, m)
            seen.enter_loop()
            with act.Fori(0, B) as b:
                for n in range(HEADS):
                    act.wait_ge(p_free[(n + 1) % 2], b * (HEADS // 2) + (n + 1) // 2 + PRIMED)
                    exp(b, n + 1, 0)
                    exp(b, n + 1, 1)
                    for j in range(2):
                        e = n * MT + j
                        act.wait_ge(t_full, b * HEADS * MT + e + 1)
                        act.activation(pT[:, j, :], bank[5 + e % 2][:, 0:SEQ], ACT.Copy).then_inc(t_free[e % 2], 1)
                    exp(b, n + 1, 2)
                    fill_copied(b, n)
                for m in range(MT):
                    for j in range(2):
                        values(b, m, j)
                for m in range(MT):
                    seen.n[m % 2] += 1
                projected(b, 1, 1)
                seen.leave_loop()

            act.wait_ge(ln_var, 2)
            act.activation(rstd[:], mv[:, :, 1], ACT.Sqrt, bias=epsc[:]).then_inc(ln_std, 1)
            with act.Fori(0, NT // 4) as g:
                act.wait_ge(r_T, 2 * g + 1 + PRIMED)
                act.activation(xt[:, 0, :], bank[0][0:KH, :], ACT.Copy).then_inc(r_Tev, 1)
                act.wait_ge(r_ln, g + 1)
                for c in range(2):
                    last = act.activation(xn[c][:, bass.ds(g * 4, 4), 0:D], st[:], ACT.Copy)
                last.then_inc(r_copy, 1)
            act.wait_ge(r_d, 1)
            act.activation(wts[:, 1, :], wts[:, 0, :], ACT.Exp).then_inc(r_e, 1)
            for f in range(2):
                act.wait_ge(b_h, f + 1)
                act.activation(hs[:, f * FH:(f + 1) * FH], bank[f][:, 0:FH], ACT.Gelu).then_inc(b_g, 1)
            with act.Fori(0, NBLK // 2) as i:
                for u in range(2):
                    for f in range(2):
                        act.wait_ge(b_h, 4 * i + 2 * u + f + 3)
                        act.activation(hs[:, f * FH:(f + 1) * FH], bank[f][:, 0:FH], ACT.Gelu).then_inc(b_g, 1)

        @block.vector
        def _(dve):
            dve.wait_ge(s_g, 16 * 4 * GP)
            for a in range(2):
                dve.tensor_copy(g0b[:, a].rearrange("p b (i c) -> p i b c", c=3),
                                g0[:, a].rearrange("p i (b c) -> p i b c", c=3)).then_inc(t_grp, 1)
            dve.tensor_copy(g1b[:].rearrange("p b (i c) -> p i b c", c=12),
                            g1[:].rearrange("p i (b c) -> p i b c", c=12)).then_inc(t_grp, 1)
            dve.wait_ge(s_tokw, 16 * 11)
            k = 22
            for b in range(B):
                for a in range(2):
                    dve.wait_ge(t_pe, k + 1)
                    dve.tensor_tensor(h[:, b * MT + a, :], bank[k % 4][:, 0:D], bf_bc[:], ALU.add).then_inc(t_ev, 1)
                    k += 1
            dve.wait_ge(t_ev, 38)
            dve.engine_nop().then_inc(t_h, 16)

            def layer_stats(done):
                for t in range(NT + MT):
                    last = dve.bn_stats(stats[:, t, :], h[:, t, :])
                last.then_inc(ln_chain, 1)
                dve.wait_ge(ln_chain, done)
                for t in range(NT + MT):
                    last = dve.bn_aggr(mv[:, t, :], stats[:, t, :])
                last.then_inc(ln_var, 1)
                dve.wait_ge(ln_var, done)

            dve.wait_ge(s_txt, 16 * B)
            layer_stats(1)
            dve.wait_ge(ln_std, 1)
            dve.reciprocal(rstd[:], rstd[:]).then_inc(ln_rstd, 1)
            dve.wait_ge(ln_rstd, 1)

            for kt in range(2):
                for part in range(3):
                    dve.wait_ge(w_high, kt * 3 + part + 1)
                    cols = slice(part * DI, (part + 1) * DI)
                    dve.tensor_tensor(wq[1][:, kt, cols], staged(kt, part), wq[0][:, kt, cols].bitcast(F32), ALU.subtract).then_inc(w_split, 1)
            seen = FillCount(dve, None, *FILLS)
            highs = FillCount(dve, None, *SPLIT_FILLS)

            def high(j, b):
                dve.wait_ge(x_hi[j], highs.done(j, b) + 1)
                highs.n[j] += 1
                seen.n[j] += 1

            def full(j, b):
                dve.wait_ge(x_full[j], seen.done(j, b) + 1)
                seen.n[j] += 1

            def normalised(nth):
                for m in range(MT):
                    t = nth * MT + m
                    last = dve.tensor_scalar(xnb[:, m, :], h_flat[:, bass.ds(t * D, D)], mv[:, bass.ds(t, 1), 0:1].rearrange("p o d -> p (o d)"),
                                             rstd[:, bass.ds(t, 1)], ALU.subtract, ALU.mult)
                last.then_inc(a_xn, 1)

            def tokens(b):
                for kt in range(2):
                    high(kt, b)
                    dve.tensor_tensor(xb[1][:, kt, :], bank[kt][0:KH, 0:SEQ], xb[0][:, kt, :].bitcast(F32), ALU.subtract).then_inc(x_free[kt], 1)

            def values(b, m, j):
                if j == 1:
                    full(1, b)
                    dve.tensor_copy(v[:, m, 384:768], bank[1][:, 0:384]).then_inc(x_free[1], 1)
                else:
                    seen.n[0] += 1

            def projected(b, p, j):
                high(j, b)
                if j == 0:
                    dve.scalar_tensor_tensor(out=qT[p % 2][1][:], in0=bank[0][:, 0:SEQ], scalar=DH ** -0.5, in1=qT[p % 2][0][:].bitcast(F32),
                                             op0=ALU.mult, op1=ALU.subtract).then_inc(x_free[0], 1)
                else:
                    for i, rows in ((0, slice(0, DH)), (1, slice(DH, P))):
                        last = dve.tensor_tensor(kz[p % 2][i][1][rows, :], bank[1][rows, 0:SEQ], kz[p % 2][i][0][rows, :].bitcast(F32), ALU.subtract)
                    last.then_inc(x_free[1], 1)

            def fill_copied(b, n):
                if n <= 7:
                    projected(b, n // 2 + 2, n % 2)
                elif n == 8:
                    tokens(b)
                elif n == 9:
                    projected(b, 0, 0)
                    projected(b, 0, 1)
                elif n == 10:
                    projected(b, 1, 0)

            def row_max(b, n, m):
                dve.wait_ge(s_full, b * HEADS * MT + n * MT + m + 1)
                dve.tensor_reduce(nmax[:, n % 2, m:m + 1], bank[2 + m][:, 0:SEQ], AX_X, ALU.max, negate=True).then_inc(s_max, 1)

            def pair_copied(b, p):
                dve.wait_ge(o_full, b * NPAIR + p + 1)
                dve.tensor_copy(oT[:, p, :], bank[7][:, 0:SEQ]).then_inc(o_free, 1)

            def normalise(b, n):
                for m in range(MT):
                    dve.wait_ge(exp_done[m], b * HEADS + n + 1 + PRIMED)
                dve.reciprocal(rinv[:, n % 2, :], rsum[:, n % 2, :]).then_inc(r_ready, 1)
                dve.wait_ge(r_ready, b * HEADS + n + 1)
                for m in range(MT):
                    last = dve.tensor_scalar(pr[n % 2][:, m, :], pr[n % 2][:, m, :], rinv[:, n % 2, m:m + 1], None, ALU.mult)
                last.then_inc(p_ready, 1)

            normalised(0)
            tokens(0)
            for m in range(MT):
                for j in range(2):
                    values(0, m, j)
            projected(0, 0, 0)
            projected(0, 0, 1)
            projected(0, 1, 0)
            projected(0, 1, 1)
            for m in range(MT):
                row_max(0, 0, m)
            normalise(0, 0)
            seen.enter_loop()
            highs.enter_loop()
            with dve.Fori(0, B) as b:
                for n in range(HEADS):
                    p = n // 2
                    for m in range(MT):
                        row_max(b, n + 1, m)
                    if n % 2 == 0 and n > 0:
                        pair_copied(b, p - 1)
                    e = n * MT + 2
                    dve.wait_ge(t_full, b * HEADS * MT + e + 1)
                    dve.tensor_copy(pT[:, 2, :], bank[5 + e % 2][:, 0:SEQ]).then_inc(t_free[e % 2], 1)
                    normalise(b, n + 1)
                    fill_copied(b, n)
                    if n == 6:
                        normalised(b + 1)
                pair_copied(b, NPAIR - 1)
                for m in range(MT):
                    for j in range(2):
                        values(b, m, j)
                for m in range(MT):
                    full(m % 2, b)
                    t = b * MT + m
                    dst_ = h_flat[:, bass.ds(t * D, D)]
                    dve.tensor_tensor(dst_, dst_, bank[m % 2][:, 0:D], ALU.add).then_inc(x_free[m % 2], 1)
                projected(b, 1, 1)
                seen.leave_loop()
                highs.leave_loop()
            for j in range(2):
                dve.wait_ge(x_free[j], FILLS[0][j] + B * FILLS[1][j] + PRIMED)
            dve.wait_ge(p_ready, B * HEADS + 1)
            dve.engine_nop().then_inc(h_done, B * MT)

            layer_stats(2)
            dve.wait_ge(ln_std, 2)
            dve.reciprocal(rstd[:], rstd[:]).then_inc(ln_rstd, 1)
            dve.wait_ge(ln_rstd, 2)
            with dve.Fori(0, NT // 4) as g:
                dve.wait_ge(r_T, 2 * g + PRIMED)
                dve.wait_ge(r_copy, g + PRIMED)
                for j in range(4):
                    t = g * 4 + j
                    last = dve.tensor_scalar(st[:, j, :], h_flat[:, bass.ds(t * D, D)], mv[:, bass.ds(t, 1), 0:1].rearrange("p o d -> p (o d)"),
                                             rstd[:, bass.ds(t, 1)], ALU.subtract, ALU.mult)
                last.then_inc(r_ln, 1)
                dve.wait_ge(r_T, 2 * g + 2 + PRIMED)
                dve.tensor_copy(xt[:, 1, :], bank[1][0:KH, :]).then_inc(r_Tev, 1)
                dve.wait_ge(r_log, g + 1)
                dve.tensor_copy(logits[:, bass.ds(g * 4, 4), :].rearrange("p t e -> p (t e)"), bank[2][:, 0:4 * E]).then_inc(r_logev, 1)
            dve.wait_ge(r_logev, NT // 4 + PRIMED)

            steps = [0]

            def step(instruction):
                steps[0] += 1
                instruction.then_inc(r_chain, 1)
                dve.wait_ge(r_chain, steps[0])

            for t in range(NT):
                last = dve.max(mx8[:, t, :], logits[:, t, :])
            step(last)
            for t in range(NT):
                last = dve.max_index(ix8[:, t, :], mx8[:, t, :], logits[:, t, :])
            step(last)
            dve.tensor_tensor(wts[:, 0, :], mx8[:, :, 1], mx8[:, :, 0], ALU.subtract).then_inc(r_d, 1)
            dve.wait_ge(s_attw, 16 * 11)
            for c in range(2):
                last = dve.tensor_copy(ixf[:, c, :], ix8[:, :, c])
            step(last)
            for c in range(2):
                last = dve.tensor_tensor(m01[:, c], eo[:], ixf[:, c:c + 1, :].broadcast_to([P, E, NT]), ALU.is_equal)
            step(last)
            dve.tensor_tensor(msum[:], m01[:, 0].rearrange("p e t -> p (e t)"), m01[:, 1].rearrange("p e t -> p (e t)"), ALU.add).then_inc(r_m, 1)
            dve.wait_ge(r_e, 1)
            step(dve.tensor_scalar(wts[:, 0, :], wts[:, 1, :], 1.0, None, ALU.add))
            step(dve.reciprocal(wts[:, 0, :], wts[:, 0, :]))
            step(dve.tensor_tensor(wts[:, 1, :], wts[:, 1, :], wts[:, 0, :], ALU.mult))
            for c in range(2):
                dve.tensor_copy(xn[c][:, :, D + 1], wts[:, c, :])
                last = dve.tensor_copy(xn[c][:, :, D].bitcast(I32), dest[:, c, :])
            step(last)
            dve.wait_ge(r_cnt, 1)
            step(dve.tensor_copy(tot[:], bank[1][:, 0:E * NT]))
            step(dve.tensor_tensor_scan(inc[:], kp[:], tot[:], 0.0, ALU.mult, ALU.add))
            n_e = inc[:].rearrange("p (e t) -> p e t", e=E)[:, :, NT - 1]
            step(dve.tensor_scalar(nbi[:], n_e, float(P - 1), None, ALU.add))
            step(dve.tensor_scalar(nbi[:], nbi[:], 7, None, ALU.logical_shift_right))
            step(dve.tensor_copy(nbf[:], nbi[:]))
            step(dve.tensor_tensor_scan(binc[:], ones[:, 0:E], nbf[:], 0.0, ALU.mult, ALU.add))
            step(dve.tensor_tensor(base[:], binc[:], nbf[:], ALU.subtract))
            step(dve.tensor_scalar(base[:], base[:], float(P), None, ALU.mult))
            step(dve.tensor_tensor(inc[:], inc[:], tot[:], ALU.subtract))
            step(dve.tensor_tensor(inc[:], inc[:], bank[0][:, 0:E * NT], ALU.add))
            inc3 = inc[:].rearrange("p (e t) -> p e t", e=E)
            step(dve.tensor_tensor(inc3, inc3, base[:].rearrange("p (e o) -> p e o", o=1).broadcast_to([P, E, NT]), ALU.add))
            for c in range(2):
                step(dve.tensor_tensor(tmp[:], inc[:], m01[:, c].rearrange("p e t -> p (e t)"), ALU.mult))
                step(dve.tensor_reduce(slotf[:, c, :], tmp[:].rearrange("p (e t) -> p t e", e=E), AX_X, ALU.add))
            dve.tensor_copy(sloti[:], slotf[:]).then_inc(r_slot, 1)
            step(dve.tensor_tensor(bcmp[:], binc[0:1, :].rearrange("p (o e) -> p o e", o=1).broadcast_to([1, NBLK_LOADED, E]), bn[:], ALU.is_le))
            step(dve.tensor_reduce(bexf[:], bcmp[:], AX_X, ALU.add))
            step(dve.tensor_scalar(bexf[:], bexf[:], float(E - 1), None, ALU.min))
            step(dve.tensor_copy(bex[:], bexf[:]))
            dve.engine_nop().then_inc(r_blk, 1)

            def block_copy(u, it):
                dve.wait_ge(b_x, 2 * it + u + 1)
                dve.tensor_copy(xT[u][0:KH, :, :], bank[6][0:KH, 0:2 * P].rearrange("p (k n) -> p k n", k=2)).then_inc(b_xev, 1)

            def address_copy(u, it):
                dve.wait_ge(b_load[u], 16 * (it + 1))
                dve.tensor_copy(dst_next[u][:].bitcast(I32), xr[u][:, D:ROW].bitcast(I32)).then_inc(b_addr, 1)

            dve.wait_ge(s_moew, 64)
            for u in range(2):
                block_copy(u, 0)
                address_copy(u, 0)
            with dve.Fori(0, NBLK // 2) as i:
                ex = [dve.value_load(bex[0:1, bass.ds(2 * i + u, 1)], min_val=0, max_val=E - 1) for u in range(2)]
                for u in range(2):
                    for f in range(2):
                        dve.wait_ge(b_t, 4 * i + 2 * u + f + 1)
                        dve.tensor_copy(hT[:, 3 * f:3 * f + 3, :].rearrange("p a b -> p (a b)"), bank[2 + f][:, 0:FH]).then_inc(b_tev, 1)
                    block_copy(u, i + 1)
                    dve.wait_ge(y_free[u], i + PRIMED)
                    dve.wait_ge(b_addr, 2 * i + u + 1)
                    dve.tensor_copy(dst[u][:].bitcast(I32), dst_next[u][:].bitcast(I32)).then_inc(b_dst, 1)
                    dve.wait_ge(b_y, 2 * i + u + 1)
                    dve.tensor_tensor(yv[u][:], bank[4 + u][:, 0:D], bo_bc[:, bass.ds(ex[u] * D, D)], ALU.add).then_inc(b_yev, 1)
                    dve.wait_ge(b_yev, 2 * i + u + 1 + PRIMED)
                    dve.wait_ge(b_dst, 2 * i + u + 1)
                    dve.tensor_scalar(yv[u][:], yv[u][:], dst[u][:, 1:2], None, ALU.mult).then_inc(b_yw, 1)
                    address_copy(u, i + 1)

            for b in range(B):
                dve.wait_ge(z_load[b % 2], 32 * (b // 2 + 1))
                hb = h[:, b * MT:(b + 1) * MT, :]
                dve.tensor_tensor(hb, hb, zc[0][b % 2][:], ALU.add).then_inc(z_chain, 1)
                dve.wait_ge(z_chain, b + 1)
                dve.tensor_tensor(hb, hb, zc[1][b % 2][:], ALU.add).then_inc(z_sum, 1)


def interpolation(n_in, n_out):
    pos = (np.arange(n_out, dtype=np.float32) + np.float32(0.5)) * np.float32(n_in / n_out) - np.float32(0.5)
    pos = np.clip(pos, 0.0, n_in - 1).astype(np.float32)
    lo = np.floor(pos).astype(np.int64)
    hi = np.minimum(lo + 1, n_in - 1)
    w = (pos - lo).astype(np.float32)
    m = np.zeros((n_in, n_out), np.float32)
    m[lo, np.arange(n_out)] += np.float32(1.0) - w
    m[hi, np.arange(n_out)] += w
    return m


def shape_constants():
    a1 = interpolation(64, TOK_IMG)
    a2 = interpolation(16, TOK_IMG)
    big = np.zeros((P, B, TOK_IMG), np.float32)
    for b in range(B):
        big[16 * b:16 * b + 16, b] = a2
    p = np.arange(P)
    dest = np.stack([c * NTOK + np.arange(NT)[None, :] * P + p[:, None] for c in range(2)], 1).astype(np.int32)
    xg = np.zeros((NBLK_LOADED * P, ROW), np.float32)
    xg[:, D] = (2 * NTOK + np.arange(NBLK_LOADED * P)).astype(np.int32).view(np.float32)
    return {
        "base2": np.repeat((256 * (p // 16)).astype(np.int32)[:, None], GP, 1),
        "ident_c": np.eye(P, dtype=np.float32),
        "tri_c": np.triu(np.ones((P, P), np.float32), 1),
        "A1": a1, "A2": big,
        "expert_of": np.broadcast_to(np.arange(E, dtype=np.float32)[None, :, None], (P, E, NT)).copy(),
        "keep": np.broadcast_to((np.arange(E * NT) % NT != 0).astype(np.float32), (P, E * NT)).copy(),
        "block_no": np.broadcast_to(np.arange(NBLK_LOADED, dtype=np.float32)[None, :, None], (1, NBLK_LOADED, E)).copy(),
        "dest_c": dest,
        "xg_init": xg,
    }


def kernel(x, txt, L0_tok_W0, L0_tok_b0, L0_tok_W1, L0_tok_b1, L0_tok_W2, L0_tok_b2, L0_tok_Wf, L0_tok_bf,
           L0_tok_idx0, L0_tok_idx1, L0_tok_idx2, L0_attn_w_qkv, L0_attn_w_o, L0_ffn_Wr, L0_ffn_Wi, L0_ffn_bi,
           L0_ffn_Wo, L0_ffn_bo):
    import concourse.bacc as bacc
    from concourse.bass_utils import run_bass_kernel_spmd

    x = np.asarray(x)

    def patches(p):
        n = IMG // p
        return x.reshape(B, CH, n, p, n, p).transpose(2, 4, 0, 3, 5, 1)

    def halves(w):
        return w.reshape(2, KH, -1).transpose(1, 0, 2)

    a = np.asarray
    arrays = {
        "xp0": patches(1).reshape(4096, B * 3),
        "xp1": patches(2).reshape(1024, B * 12),
        "xp2": patches(4).transpose(2, 0, 1, 3, 4, 5).reshape(B * 256, 48),
        "txt": a(txt),
        "W0T": a(L0_tok_W0).T, "b0": a(L0_tok_b0).reshape(-1, 1),
        "W1T": a(L0_tok_W1).T.reshape(2, 96, EMB).transpose(1, 0, 2), "b1": a(L0_tok_b1).reshape(-1, 1),
        "W2T": a(L0_tok_W2).T.reshape(8, 96, EMB).transpose(1, 0, 2), "b2": a(L0_tok_b2).reshape(-1, 1),
        "WfT": a(L0_tok_Wf).T, "bf": a(L0_tok_bf).reshape(1, -1),
        "idx0": a(L0_tok_idx0), "idx1": a(L0_tok_idx1), "idx2": a(L0_tok_idx2),
        "wqkv": halves(a(L0_attn_w_qkv).transpose(2, 1, 0, 3).reshape(D, 3 * DI)),
        "wo": a(L0_attn_w_o).reshape(NPAIR, P, D).transpose(1, 0, 2),
        "WrT": halves(a(L0_ffn_Wr).T),
        "WiT": halves(a(L0_ffn_Wi).transpose(2, 0, 1).reshape(D, E * F)),
        "bi": a(L0_ffn_bi).reshape(1, -1),
        "WoT": a(L0_ffn_Wo).transpose(0, 2, 1).reshape(E * FT, P, D).transpose(1, 0, 2),
        "bo": a(L0_ffn_bo).reshape(1, -1),
    }
    arrays.update(shape_constants())
    nc = bacc.Bacc("TRN2", target_bir_lowering=False, num_devices=1)
    given, aps = {}, {}
    for name, value in arrays.items():
        value = np.ascontiguousarray(value)
        given["in_" + name] = value
        aps[name] = nc.dram_tensor("in_" + name, value.shape, mybir.dt.from_np(value.dtype), kind="ExternalInput").ap()
    aps["xg"] = nc.dram_tensor("routed_rows", (NBLK_LOADED * P, ROW), F32, kind="Internal").ap()
    aps["z"] = nc.dram_tensor("routed_results", (2 * NTOK + NBLK_LOADED * P, D), F32, kind="Internal").ap()
    aps["out"] = nc.dram_tensor("out_0", (B, SEQ, D), F32, kind="ExternalOutput").ap()
    fused_layer_kernel(nc, **aps)
    result = run_bass_kernel_spmd(nc, [given], core_ids=[0])
    return result.results[0]["out_0"]
```

```python
from contextlib import ExitStack

import numpy as np
import concourse.bass as bass
from concourse import mybir

F32 = mybir.dt.float32
F32R = mybir.dt.float32r
I32 = mybir.dt.int32
U32 = mybir.dt.uint32
ALU = mybir.AluOpType
ACT = mybir.ActivationFunctionType
AX_X = mybir.AxisListType.X

P = 128
B = 8
IMG, CH, GP = 64, 3, 16
G1, G2 = 8, 2
TOK_IMG = IMG * IMG // GP
TOK_TXT = 128
SEQ = TOK_IMG + TOK_TXT
D = 192
KH = D // 2
MT = SEQ // P
NT = B * MT
NTOK = NT * P
HEADS, DH = 12, 64
NPAIR = HEADS // 2
DI = HEADS * DH
EMB = 64
E = 8
F = 768
FT = F // P
FH = F // 2
REGION = NTOK + P
NBLK = 2 * NT + E
NBLK_LOADED = NBLK + 4
SPARE = NBLK_LOADED - 2 * NT
SLOTS = E * REGION + SPARE * P
ROW = D + 2
EPS = 1e-5
PRIMED = 1


class FillCount:

    per_batch = (14, 13)

    def __init__(self, engine, free=None):
        self.engine, self.free = engine, free
        self.n, self.step_start, self.before = [0, 0], [0, 0], None

    def enter_loop(self):
        self.before, self.n = self.n, [0, 0]

    def leave_loop(self):
        self.n = [self.before[j] + (B - 2) * self.n[j] for j in range(2)]
        self.before = None

    def count(self, j, b, n, per_batch):
        return n if self.before is None else (b - 1) * per_batch[j] + self.before[j] + n

    def done(self, j, b):
        return self.count(j, b, self.n[j], self.per_batch)

    def next(self, j, b):
        self.engine.wait_ge(self.free[j], self.done(j, b) + PRIMED)
        self.n[j] += 1
        return j

    def settled(self, b):
        for j in range(2):
            self.engine.wait_ge(self.free[j], self.done(j, b) + PRIMED)

    def settled_before_step(self, b):
        for j in range(2):
            self.engine.wait_ge(self.free[j], self.count(j, b, self.step_start[j], self.per_batch) + PRIMED)


class SplitCount(FillCount):
    per_batch = (7, 7)


def fused_layer_kernel(nc, xp0, xp1, xp2, txt, W0T, b0, W1T, b1, W2T, b2, WfT, bf, idx0, idx1, idx2,
                       wqkv, wo, WrT, WiT, bi, WoT, bo, ident_c, tri_c, A1, A2, expert_of,
                       region_c, block_no, dest_c, pad_rows, spare_rows, xg, z, out):
    ctx = ExitStack()

    def sb(stack, name, shape, dt=F32):
        return stack.enter_context(nc.sbuf_tensor(name, shape, dt))

    def sem(name):
        return ctx.enter_context(nc.semaphore(name))

    with ctx:
        h = sb(ctx, "h", [P, NT, D])
        wi = sb(ctx, "wi", [KH + 1, 2, E * F])
        ident = sb(ctx, "ident", [P, P])
        tri = sb(ctx, "tri", [P, P])
        ones = sb(ctx, "ones", [P, P])
        wr = sb(ctx, "wr", [KH, 2, E])
        epsc = sb(ctx, "epsc", [P, 1])
        unused = sb(ctx, "unused", [P, 1])
        stats = sb(ctx, "stats", [P, NT, 6])
        mv = sb(ctx, "mv", [P, NT, 2])
        rstd = sb(ctx, "rstd", [P, NT])
        dest = sb(ctx, "dest", [P, 2, NT], I32)
        eo = sb(ctx, "eo", [P, E, MT])
        nxt = sb(ctx, "nxt", [P, E])
        bn = sb(ctx, "bn", [1, NBLK_LOADED, E])
        bex = sb(ctx, "bex", [1, NBLK_LOADED], I32)
        brow = sb(ctx, "brow", [1, NBLK_LOADED], I32)

        tk = ExitStack()
        i0 = sb(tk, "i0", [P, 2, GP], I32)
        i1 = sb(tk, "i1", [P, G1], I32)
        i2 = sb(tk, "i2", [P, G2], I32)
        g0 = sb(tk, "g0", [P, 2, GP, B * 3])
        g1 = sb(tk, "g1", [P, G1, B * 12])
        g2 = sb(tk, "g2", [P, G2, B * 48])
        g0b = sb(tk, "g0b", [P, 2, B, GP * 3])
        g1b = sb(tk, "g1b", [P, B, G1 * 12])
        g2b = sb(tk, "g2b", [P, B, G2 * 48])
        g0t = sb(tk, "g0t", [48, B * P])
        g1t = sb(tk, "g1t", [96, B, P])
        g2t = sb(tk, "g2t", [96, 8, P])
        e1 = sb(tk, "e1", [64, 512])
        e2 = sb(tk, "e2", [P, EMB])
        ya = sb(tk, "ya", [P, B * TOK_IMG])
        yb = sb(tk, "yb", [EMB, B * TOK_IMG])
        a1 = sb(tk, "a1", [64, TOK_IMG])
        a2 = sb(tk, "a2", [P, B, TOK_IMG])
        tk.close()

        ro = ExitStack()
        rows = [sb(ro, f"rows{c}", [P, MT, ROW]) for c in range(2)]
        xt = sb(ro, "xt", [KH, 2, SEQ])
        mv2 = sb(ro, "mv2", [P, MT, 2])
        rs = sb(ro, "rs", [P, 3, MT])
        rsi = sb(ro, "rsi", [P, MT], I32)
        logits = sb(ro, "logits", [P, MT, E])
        mx8 = sb(ro, "mx8", [P, MT, 8])
        ix8 = sb(ro, "ix8", [P, MT, 8], U32)
        ixf = sb(ro, "ixf", [P, 2, MT])
        m01 = sb(ro, "m01", [P, 2, E, MT])
        msum = sb(ro, "msum", [P, E * MT])
        rank = sb(ro, "rank", [P, 2, E * MT])
        sloti = sb(ro, "sloti", [P, 2, MT], I32)
        wts = sb(ro, "wts", [P, 2, MT])
        tmp = sb(ro, "tmp", [P, 2, E * MT])
        base = sb(ro, "base", [P, E])
        nbi = sb(ro, "nbi", [P, E], I32)
        nbf = sb(ro, "nbf", [P, E])
        binc = sb(ro, "binc", [P, E])
        ends = sb(ro, "ends", [1, E], I32)
        pads = sb(ro, "pads", [P, E, ROW])
        bcmp = sb(ro, "bcmp", [1, NBLK_LOADED, E])
        bexf = sb(ro, "bexf", [1, NBLK_LOADED])

        at = ExitStack()
        xnb = sb(at, "xnb", [P, MT, D])
        xb = [sb(at, f"xb{s}", [KH, 2, SEQ], F32R) for s in range(2)]
        qT = [[sb(at, f"qT{i}{s}", [P, SEQ], F32R) for s in range(2)] for i in range(2)]
        kz = [[[sb(at, f"kz{i}{j}{s}", [P, SEQ], F32R) for s in range(2)] for j in range(2)] for i in range(2)]
        pr = [sb(at, f"pr{i}", [P, MT, SEQ]) for i in range(2)]
        pT = sb(at, "pT", [P, MT, SEQ])
        nmax = sb(at, "nmax", [P, 2, MT])
        rsum = sb(at, "rsum", [P, 2, MT])
        rinv = sb(at, "rinv", [P, 2, MT])
        wot = sb(at, "wot", [P, NPAIR, D])
        wq = [sb(at, f"wq{s}", [KH, 2, 3 * DI], F32R) for s in range(2)]
        v = sb(at, "v", [P, MT, DI])
        oT = sb(at, "oT", [P, NPAIR, SEQ])
        w0 = sb(at, "w0", [48, EMB])
        w1 = sb(at, "w1", [96, 2, EMB])
        w2 = sb(at, "w2", [96, 8, EMB])
        wfa = sb(at, "wfa", [P, D])
        wfb = sb(at, "wfb", [EMB, D])
        bca = sb(at, "bca", [P, 1])
        bcb = sb(at, "bcb", [EMB, 1])
        bf_bc = sb(at, "bf_bc", [P, D])
        at.close()

        re = ExitStack()
        zc = [[sb(re, f"z{c}{b}", [P, MT, D]) for b in range(B)] for c in range(2)]
        re.close()

        mo = ExitStack()
        wo2 = sb(mo, "wo2", [P, E * FT, D])
        bo_bc = sb(mo, "bo_bc", [P, E * D])
        xr = [sb(mo, f"xr{u}", [P, ROW]) for u in range(2)]
        dst = [sb(mo, f"dst{u}", [P, 2]) for u in range(2)]
        dst_next = [sb(mo, f"dst_next{u}", [P, 2]) for u in range(2)]
        xT = [[sb(mo, f"xT{u}{s}", [KH + 1, 2, P], F32R) for s in range(2)] for u in range(2)]
        wih = sb(mo, "wih", [KH + 1, 2, E * F], F32R)
        hs = sb(mo, "hs", [P, F])
        hT = sb(mo, "hT", [P, FT, P])
        yv = [sb(mo, f"yv{u}", [P, D]) for u in range(2)]
        mo.close()
        ro.close()

        bank = [ctx.enter_context(nc.psum_tensor(f"bank{i}", [P, 512], F32)) for i in range(8)]

        s_idx = [sem(f"indices{level}_loaded") for level in range(3)]
        s_const, s_tokw, s_txt, s_moew = map(sem, (
            "constants_loaded",
            "tokenizer_weights_loaded", "text_loaded", "expert_weights_loaded"))
        s_attw, s_xginit = sem("attention_weights_loaded"), sem("slots_initialised")
        s_setup = sem("constants_set")
        s_g1, s_g2 = sem("patches1_gathered"), sem("patches2_gathered")
        s_g0 = [sem("patches0_gathered0"), sem("patches0_gathered1")]
        s_wot, s_upw = sem("output_weights_loaded"), sem("up_weights_loaded")
        t_grp = sem("patches_regrouped")
        t_pe, t_ev, t_h = sem("tokenizer_product_ready"), sem("tokenizer_product_copied"), sem("image_tokens_ready")
        ln_chain, ln_var, ln_std, ln_rstd = sem("ln_dve_step"), sem("variances_ready"), sem("std_ready"), sem("rstd_ready")
        a_xn = sem("batch_normalised")
        x_full = [sem("projection0_ready"), sem("projection1_ready")]
        x_hi = [sem("projection0_high_part_ready"), sem("projection1_high_part_ready")]
        w_split, w_high = sem("attention_weights_split"), sem("attention_weights_high_parts")
        x_free = [sem("projection0_copied"), sem("projection1_copied")]
        s_full, s_max, exp_done = sem("scores_ready"), sem("max_ready"), [sem(f"exp_done{m}") for m in range(MT)]
        r_ready, p_ready, p_free = sem("sum_inverted"), sem("probs_ready"), [sem("probs0_used"), sem("probs1_used")]
        t_full, t_free = sem("probs_transposed"), [sem("transpose0_copied"), sem("transpose1_copied")]
        o_full, o_free = sem("head_pair_ready"), sem("head_pair_copied")
        h_done = sem("attention_added")
        r_ln, r_copy, r_gap, r_exp, r_masks, r_slot, r_free, r_end, r_blk = map(sem, (
            "router_input_ready", "routed_rows_copied", "logit_gap_ready", "gap_exp_ready", "choice_masks_ready",
            "slots_ready", "routed_rows_free", "pad_slots_ready", "block_experts_ready"))
        r_chain, r_pool = sem("router_dve_step"), sem("router_pool_step")
        r_var, r_rstd, r_ranks = sem("router_variances_ready"), sem("router_rstd_ready"), sem("ranks_copied")
        s_scat, s_pads = sem("rows_scattered"), sem("padding_scattered")
        s_rconst, s_rpad = sem("router_constants_loaded"), sem("padding_rows_loaded")
        e_high, e_split, b_xhi = sem("up_weights_high_parts"), sem("up_weights_split"), sem("block_transpose_high_part_ready")
        b_load = [sem("block_loaded0"), sem("block_loaded1")]
        b_x, b_xev, b_h, b_g, b_t, b_tev, b_y, b_yev, b_yw = map(sem, (
            "block_transposed", "block_transpose_copied", "hidden_ready", "gelu_done", "hidden_transposed",
            "hidden_transpose_copied", "expert_out_ready", "expert_bias_added", "expert_out_weighted"))
        b_addr, b_dst = sem("next_addresses_copied"), sem("addresses_ready")
        y_free = [sem("result0_free"), sem("result1_free")]
        b_scat = [sem("result_scattered0"), sem("result_scattered1")]
        z_load = [sem(f"results_loaded{b}") for b in range(B)]
        z_chain, z_sum, z_out = sem("first_result_added"), sem("output_tile_ready"), sem("output_stored")

        primed = [*x_free, *exp_done, *p_free, *t_free, o_free, r_free, b_xev, b_tev, b_yev, *y_free]

        block = ctx.enter_context(nc.Block())
        h_flat = h[:].rearrange("p t d -> p (t d)")

        def routed_results(c, b):
            return z[c * NTOK + b * SEQ:c * NTOK + (b + 1) * SEQ, :].rearrange("(m p) d -> p m d", p=P)

        def staged(kt, part):
            if kt == 0:
                return oT[0:KH, 2 * part:2 * part + 2, :].rearrange("p a b -> p (a b)")
            return v[0:KH, part, :]

        @block.sync
        def _(sp):
            for a in range(GP // G1):
                sp.dma_start(i1[64 * a:64 * a + 64, :], idx1.rearrange("(t a j) -> a t j", j=G1, t=64)[a]).then_inc(s_idx[1], 16)
            for a in range(GP // G2):
                sp.dma_start(i2[16 * a:16 * a + 16, :], idx2.rearrange("(t a j) -> a t j", j=G2, t=16)[a]).then_inc(s_idx[2], 16)
            sp.dma_start(i0[:], idx0.rearrange("(a t i) -> t a i", a=2, i=GP)).then_inc(s_idx[0], 16)
            for dst_, src in ((ident, ident_c), (tri, tri_c), (wr, WrT)):
                sp.dma_start(dst_[:], src).then_inc(s_const, 16)
            for dst_, src in ((w0, W0T), (w1, W1T), (w2, W2T), (a1, A1), (a2, A2)):
                sp.dma_start(dst_[:], src).then_inc(s_tokw, 16)
            sp.dma_start(wfa[:], WfT[0:P, :]).then_inc(s_tokw, 16)
            sp.dma_start(wfb[:], WfT[P:D, :]).then_inc(s_tokw, 16)
            sp.dma_start(bca[0:EMB, :], b0).then_inc(s_tokw, 16)
            sp.dma_start(bca[EMB:P, :], b1).then_inc(s_tokw, 16)
            sp.dma_start(bcb[:], b2).then_inc(s_tokw, 16)
            sp.dma_start(bf_bc[:], bf.broadcast_to([P, D])).then_inc(s_tokw, 16)
            for kt in range(2):
                for part in range(3):
                    sp.dma_start(staged(kt, part), wqkv[:, kt, part * DI:(part + 1) * DI]).then_inc(s_attw, 16)
            for b in range(B):
                sp.dma_start(h[:, b * MT + 2, :], txt[b]).then_inc(s_txt, 16)
            sp.dma_start(wi[0:KH, :, :], WiT).then_inc(s_upw, 16)
            sp.dma_start(wi[KH:KH + 1, 1, :], bi).then_inc(s_upw, 16)
            for dst_, src in ((eo, expert_of), (nxt, region_c), (bn, block_no), (dest, dest_c)):
                sp.dma_start(dst_[:], src).then_inc(s_rconst, 16)
            sp.dma_start(xg[E * REGION:SLOTS, :], spare_rows).then_inc(s_xginit, 16)
            sp.wait_ge(t_h, 16)
            sp.dma_start(wot[:], wo).then_inc(s_wot, 16)
            sp.dma_start(pads[:], pad_rows).then_inc(s_rpad, 16)
            sp.wait_ge(h_done, B * MT)
            sp.dma_start(wo2[:], WoT).then_inc(s_moew, 16)
            sp.dma_start(bo_bc[:], bo.broadcast_to([P, E * D])).then_inc(s_moew, 16)
            sp.wait_ge(s_rpad, 16)
            sp.wait_ge(r_end, 1)
            for e in range(E):
                end = sp.value_load(ends[0:1, e:e + 1], min_val=0, max_val=SLOTS - P)
                sp.dma_start(xg[bass.ds(end, P), :], pads[:, e, :]).then_inc(s_pads, 16)
            def first_slot(n):
                return sp.value_load(brow[0:1, bass.ds(n, 1)], min_val=0, max_val=SLOTS - P)

            sp.wait_ge(r_blk, 1)
            slots = [first_slot(u) for u in range(2)]
            sp.wait_ge(s_xginit, 16)
            sp.wait_ge(s_scat, 16 * 2 * NT)
            sp.wait_ge(s_pads, 16 * E)
            for u in range(2):
                sp.dma_start(xr[u][:], xg[bass.ds(slots[u], P), :]).then_inc(b_load[u], 16)
            with sp.Fori(0, NBLK // 2) as i:
                for u in range(2):
                    slot = first_slot(2 * i + 2 + u)
                    sp.wait_ge(b_x, 2 * i + u + 1)
                    sp.wait_ge(b_addr, 2 * i + u + 1)
                    sp.dma_start(xr[u][:], xg[bass.ds(slot, P), :]).then_inc(b_load[u], 16)
            for u in range(2):
                sp.wait_ge(b_scat[u], 16 * (NBLK // 2))
                sp.wait_ge(b_load[u], 16 * (NBLK // 2 + 1))
            sp.wait_ge(b_x, NBLK + 2)
            for b in range(B):
                sp.dma_start(zc[0][b][:], routed_results(0, b)).then_inc(z_load[b], 16)
            for b in range(B):
                sp.wait_ge(z_sum, b + 1)
                sp.dma_start(out[b].rearrange("(m p) d -> p m d", p=P), h[:, b * MT:(b + 1) * MT, :]).then_inc(z_out, 16)
            sp.wait_ge(z_out, 16 * B)

        @block.gpsimd
        def _(pool):
            for s in primed:
                pool.sem_inc(s, PRIMED)
            pool.memset(ones[:], 1.0).then_inc(s_setup, 1)
            pool.memset(epsc[:], EPS).then_inc(s_setup, 1)
            pool.wait_ge(s_idx[1], 16 * (GP // G1))
            for j in range(G1):
                pool.indirect_dma_start(out=g1[:, j, :], out_offset=None, in_=xp1,
                                        in_offset=bass.IndirectOffsetOnAxis(ap=i1[:, j:j + 1], axis=0)).then_inc(s_g1, 16)
            pool.wait_ge(s_idx[2], 16 * (GP // G2))
            for j in range(G2):
                pool.indirect_dma_start(out=g2[:, j, :], out_offset=None, in_=xp2,
                                        in_offset=bass.IndirectOffsetOnAxis(ap=i2[:, j:j + 1], axis=0)).then_inc(s_g2, 16)
            pool.wait_ge(s_idx[0], 16)
            for a in range(2):
                for i in range(GP):
                    pool.indirect_dma_start(out=g0[:, a, i, :], out_offset=None, in_=xp0,
                                            in_offset=bass.IndirectOffsetOnAxis(ap=i0[:, a, i:i + 1], axis=0)).then_inc(s_g0[a], 16)
            pool.wait_ge(t_h, 16)
            pool.wait_ge(s_setup, 2)
            for i in range(2):
                for s in range(2):
                    pool.memset(kz[i][0][s][DH:P, :].bitcast(F32), 0.0).then_inc(s_setup, 1)
                    pool.memset(kz[i][1][s][0:DH, :].bitcast(F32), 0.0).then_inc(s_setup, 1)
            POOL_STEPS = 14 + 10
            v_, y, q = (rs[:, i, :] for i in range(3))
            steps = [0]

            def step(instruction, r):
                steps[0] += 1
                instruction.then_inc(r_pool, 1)
                pool.wait_ge(r_pool, r * POOL_STEPS + steps[0])
                pool.nop(nofuse=True)

            def route_rstd(r):
                steps[0] = 0
                pool.wait_ge(r_var, r + 1)
                pool.nop(nofuse=True)
                step(pool.tensor_scalar(v_, mv2[:, :, 1], EPS, None, ALU.add), r)
                step(pool.tensor_scalar(rsi[:], v_.bitcast(I32), -0.5, float(0x5f3759df), ALU.mult, ALU.add), r)
                for it in range(3):
                    guess = rsi[:].bitcast(F32) if it == 0 else y
                    step(pool.tensor_tensor(q, guess, guess, ALU.mult), r)
                    step(pool.tensor_tensor(q, q, v_, ALU.mult), r)
                    step(pool.tensor_scalar(q, q, -0.5, 1.5, ALU.mult, ALU.add), r)
                    step(pool.tensor_tensor(y, guess, q, ALU.mult), r)
                pool.engine_nop().then_inc(r_rstd, 1)

            def route_slots(r):
                pool.wait_ge(r_ranks, r + 1)
                pool.nop(nofuse=True)
                slot3, count3 = (rank[:, i, :].rearrange("p (e t) -> p e t", e=E) for i in range(2))
                for t in range(MT):
                    step(pool.tensor_tensor(slot3[:, :, t], slot3[:, :, t], nxt[:], ALU.add), r)
                    step(pool.tensor_tensor(nxt[:], nxt[:], count3[:, :, t], ALU.add), r)
                for c in range(2):
                    last = pool.tensor_tensor(tmp[:, c, :], rank[:, 0, :], m01[:, c].rearrange("p e t -> p (e t)"), ALU.mult)
                step(last, r)
                for half in (E * MT // 2, E * MT // 4, E * MT // 8):
                    step(pool.tensor_tensor(tmp[:, :, 0:half], tmp[:, :, 0:half], tmp[:, :, half:2 * half], ALU.add), r)
                pool.tensor_copy(sloti[:], tmp[:, :, 0:MT]).then_inc(r_slot, 1)
                assert steps[0] == POOL_STEPS

            def scatter_rows(r):
                pool.wait_ge(r_copy, r + 1)
                pool.wait_ge(r_slot, r + 1)
                pool.nop(nofuse=True)
                for c in range(2):
                    for m in range(MT):
                        pool.indirect_dma_start(out=xg, out_offset=bass.IndirectOffsetOnAxis(ap=sloti[:, c, m:m + 1], axis=0),
                                                in_=rows[c][:, m, :], in_offset=None).then_inc(s_scat, 16)
                pool.wait_ge(s_scat, 16 * 2 * MT * (r + 1) if isinstance(r, int) else r * (16 * 2 * MT) + 16 * 2 * MT)
                pool.sem_inc(r_free, 1)

            with pool.Fori(1, B) as b:
                route_rstd(b - 1)
                route_slots(b - 1)
                scatter_rows(b - 1)
            route_rstd(B - 1)
            route_slots(B - 1)
            scatter_rows(B - 1)
            pool.wait_ge(h_done, B * MT)
            for u in range(2):
                pool.memset(xT[u][0][KH:KH + 1, 1, :].bitcast(F32), 1.0).then_inc(s_setup, 1)
                pool.memset(xT[u][1][KH:KH + 1, 1, :].bitcast(F32), 0.0).then_inc(s_setup, 1)
            with pool.Fori(0, NBLK // 2) as i:
                for u in range(2):
                    pool.wait_ge(b_yw, 2 * i + u + 1)
                    pool.nop(nofuse=True)
                    pool.indirect_dma_start(out=z, out_offset=bass.IndirectOffsetOnAxis(ap=dst[u][:, 0:1].bitcast(I32), axis=0),
                                            in_=yv[u][:], in_offset=None).then_inc(b_scat[u], 16)
                    pool.wait_ge(b_scat[u], 16 * (i + 1))
                    pool.sem_inc(y_free[u], 1)

        @block.tensor
        def _(pe):
            pe.wait_ge(s_const, 48)
            k = 0

            def start_product(first, needs=0):
                if max(first - 3, needs) > 0:
                    pe.wait_ge(t_ev, max(first - 3, needs))
            for level, src in ((1, g1b), (2, g2b)):
                pe.wait_ge(t_grp, level)
                for b in range(0, B, 4):
                    start_product(k)
                    for j in range(4):
                        last = pe.transpose(bank[k % 4][0:96, j * P:(j + 1) * P], src[:, b + j, :], ident[:])
                    last.then_inc(t_pe, 1)
                    k += 1
            pe.wait_ge(s_tokw, 16 * 11)
            start_product(k, 2)
            for b in range(B):
                for kt in range(2):
                    last = pe.matmul(bank[k % 4][0:64, b * 64:(b + 1) * 64], g1t[:, b, kt * 64:(kt + 1) * 64], w1[:, kt, :],
                                     start=kt == 0, stop=kt == 1)
            last.then_inc(t_pe, 1)
            k += 1
            start_product(k, 4)
            for kt in range(8):
                last = pe.matmul(bank[k % 4][:, 0:EMB], g2t[:, kt, :], w2[:, kt, :], start=kt == 0, stop=kt == 7)
            last.then_inc(t_pe, 1)
            k += 1
            for b in range(0, B, 2):
                start_product(k, 5)
                for j in range(2):
                    last = pe.matmul(bank[k % 4][EMB:P, j * TOK_IMG:(j + 1) * TOK_IMG],
                                     e1[:, (b + j) * 64:(b + j + 1) * 64], a1[:], start=True, stop=True)
                last.then_inc(t_pe, 1)
                k += 1
            for b in range(0, B, 2):
                start_product(k)
                for j in range(2):
                    last = pe.matmul(bank[k % 4][0:EMB, j * TOK_IMG:(j + 1) * TOK_IMG],
                                     e2[:], a2[:, b + j, :], start=True, stop=True)
                last.then_inc(t_pe, 1)
                k += 1
            for a in range(2):
                pe.wait_ge(t_grp, 3 + a)
                for b in range(0, B, 4):
                    start_product(k)
                    for j in range(4):
                        last = pe.transpose(bank[k % 4][0:48, j * P:(j + 1) * P], g0b[:, a, b + j, :], ident[:])
                    last.then_inc(t_pe, 1)
                    k += 1
                for b in range(0, B, 4):
                    start_product(k, k - 1)
                    pe.matmul(bank[k % 4][0:EMB, :], w0[:], g0t[:, b * P:(b + 4) * P],
                              start=True, stop=True).then_inc(t_pe, 1)
                    k += 1
                for b in range(B):
                    start_product(k, k - b)
                    c0 = b * TOK_IMG + a * P
                    pe.matmul(bank[k % 4][:, 0:D], ya[:, c0:c0 + P], wfa[:], start=True, stop=False)
                    pe.matmul(bank[k % 4][:, 0:D], yb[:, c0:c0 + P], wfb[:], start=False, stop=True).then_inc(t_pe, 1)
                    k += 1

            PB = [bank[0], bank[1]]
            SB = bank[2:5]
            TB = bank[5:7]
            OB = bank[7]
            pe.wait_ge(s_wot, 16)
            pe.wait_ge(w_split, 6)
            pe.wait_ge(s_setup, 10)
            PARTS = ((0, 0), (0, 1), (1, 0))
            fills = FillCount(pe, x_free)

            def split_product(o, lhsT, rhs, kts):
                steps_ = [(kt, a, c) for kt in range(kts) for a, c in PARTS]
                for i, (kt, a, c) in enumerate(steps_):
                    last = pe.matmul(o, lhsT(kt, a), rhs(kt, c), start=i == 0, stop=i == len(steps_) - 1)
                return last

            def transpose_tokens(b, nth):
                pe.wait_ge(a_xn, nth + 1)
                for kt in range(2):
                    o = PB[fills.next(kt, b)]
                    for m in range(MT):
                        last = pe.transpose(o[0:KH, m * P:(m + 1) * P], xnb[:, m, kt * KH:(kt + 1) * KH], ident[:])
                    last.then_inc(x_full[kt], 1)

            def values(b, m, j):
                o = PB[fills.next(j, b)]
                c0 = 2 * DI + j * 384
                split_product(o[:, 0:384], lambda kt, a: xb[a][:, kt, m * P:(m + 1) * P],
                              lambda kt, c: wq[c][:, kt, c0:c0 + 384], 2).then_inc(x_full[j], 1)

            def project(b, p, j):
                o = PB[fills.next(j, b)]
                c0 = j * DI + p * P
                split_product(o[:, 0:SEQ], lambda kt, a: wq[a][:, kt, c0:c0 + P],
                              lambda kt, c: xb[c][:, kt, :], 2).then_inc(x_full[j], 1)

            def score(b, n, m):
                p = n // 2
                pe.wait_ge(exp_done[m], b * HEADS + n + PRIMED)
                split_product(SB[m][:, 0:SEQ], lambda kt, a: qT[p % 2][a][:, m * P:(m + 1) * P],
                              lambda kt, c: kz[p % 2][n % 2][c][:], 1).then_inc(s_full, 1)

            def transpose_probs(b, n, j):
                e = n * MT + j
                pe.wait_ge(t_free[e % 2], b * (HEADS * MT // 2) + e // 2 + PRIMED)
                for m in range(MT):
                    last = pe.transpose(TB[e % 2][:, m * P:(m + 1) * P], pr[n % 2][:, m, j * P:(j + 1) * P], ident[:])
                last.then_inc(t_full, 1)

            def route_transpose(b, r, kt):
                pe.wait_ge(r_ln, r + 1)
                o = PB[fills.next(kt, b)]
                for m in range(MT):
                    last = pe.transpose(o[0:KH, m * P:(m + 1) * P], rows[0][:, m, kt * KH:(kt + 1) * KH], ident[:])
                last.then_inc(x_full[kt], 1)

            def route_logits(b):
                o = PB[fills.next(0, b)]
                for m in range(MT):
                    for kt in range(2):
                        last = pe.matmul(o[:, m * E:(m + 1) * E], xt[:, kt, m * P:(m + 1) * P], wr[:, kt, :],
                                         start=kt == 0, stop=kt == 1)
                last.then_inc(x_full[0], 1)

            def route_rank(b, r):
                pe.wait_ge(r_masks, r + 1)
                o = PB[fills.next(1, b)]
                pe.matmul(o[:, 0:E * MT], tri[:], msum[:], start=True, stop=True)
                pe.matmul(o[:, E * MT:2 * E * MT], ones[:], msum[:], start=True, stop=True).then_inc(x_full[1], 1)

            def fill(b, n, more):
                fills.step_start = list(fills.n)
                if n <= 7:
                    project(b, n // 2 + 2, n % 2)
                elif not more:
                    return
                elif n == 8:
                    transpose_tokens(b, b + 1)
                elif n == 9:
                    fills.settled(b)
                    project(b, 0, 0)
                    project(b, 0, 1)
                elif n == 10:
                    project(b, 1, 0)

            def late_fill(b, n):
                if n == 5:
                    route_transpose(b, b - 1, 0)
                elif n == 6:
                    route_transpose(b, b - 1, 1)
                elif n == 7:
                    fills.settled_before_step(b)
                    route_logits(b)
                elif n == 10:
                    route_rank(b, b - 1)

            transpose_tokens(0, 0)
            fills.settled(0)
            for m in range(MT):
                for j in range(2):
                    values(0, m, j)
            project(0, 0, 0)
            project(0, 0, 1)
            project(0, 1, 0)
            project(0, 1, 1)
            fills.settled(0)
            for m in range(MT):
                score(0, 0, m)

            def batch(b, route, more):
                for n in range(HEADS):
                    p = n // 2
                    if n % 2 == 1:
                        fills.settled_before_step(b)
                    if more or n + 1 < HEADS:
                        for m in range(MT):
                            score(b, n + 1, m)
                    pe.wait_ge(p_ready, b * HEADS + n + 1)
                    transpose_probs(b, n, 0)
                    transpose_probs(b, n, 1)
                    fill(b, n, more)
                    transpose_probs(b, n, 2)
                    if n % 2 == 0:
                        pe.wait_ge(o_free, b * NPAIR + p + PRIMED)
                    for j in range(MT):
                        e = n * MT + j
                        pe.wait_ge(t_free[e % 2], b * (HEADS * MT // 2) + e // 2 + 1 + PRIMED)
                        last = pe.matmul(OB[(n % 2) * DH:(n % 2) * DH + DH, 0:SEQ], v[:, j, n * DH:(n + 1) * DH],
                                         pT[:, j, :], start=j == 0, stop=j == MT - 1)
                        if j == 0:
                            last.then_inc(p_free[n % 2], 1)
                    if n % 2 == 1:
                        last.then_inc(o_full, 1)
                    if route:
                        late_fill(b, n)
                if more:
                    for m in range(MT):
                        for j in range(2):
                            values(b, m, j)
                pe.wait_ge(o_free, b * NPAIR + NPAIR + PRIMED)
                for m in range(MT):
                    o = PB[fills.next(m % 2, b)]
                    for p in range(NPAIR):
                        last = pe.matmul(o[:, 0:D], oT[:, p, m * P:(m + 1) * P], wot[:, p, :], start=p == 0, stop=p == NPAIR - 1)
                    last.then_inc(x_full[m % 2], 1)
                if more:
                    project(b, 1, 1)

            batch(0, route=False, more=True)
            fills.enter_loop()
            with pe.Fori(1, B - 1) as b:
                batch(b, route=True, more=True)
            fills.leave_loop()
            batch(B - 1, route=True, more=False)
            for kt in range(2):
                route_transpose(B, B - 1, kt)
            fills.settled(B)
            route_logits(B)
            route_rank(B, B - 1)

            HB, TT, YB, XB = bank[0:2], bank[2:4], bank[4:6], bank[6]

            def block_transpose(n, u):
                pe.wait_ge(b_load[u], 16 * ((n - u) // 2 + 1) if isinstance(n, int) else 8 * (n - u) + 16)
                pe.wait_ge(b_xev, n + PRIMED)
                for kt in range(2):
                    last = pe.transpose(XB[0:KH, kt * P:(kt + 1) * P], xr[u][:, kt * KH:(kt + 1) * KH], ident[:])
                last.then_inc(b_x, 1)

            def hidden(n, u, expert):
                pe.wait_ge(b_xev, n + 1 + PRIMED)
                for f in range(2):
                    cols = bass.ds(expert * F + f * FH, FH)
                    for kt in range(2):
                        rows_ = slice(0, KH + kt)
                        w_ = (wih[rows_, kt, cols], wi[rows_, kt, cols].bitcast(F32R))
                        for a, c in PARTS:
                            last = pe.matmul(HB[f][:, 0:FH], xT[u][a][rows_, kt, :], w_[c],
                                             start=kt == 0 and (a, c) == PARTS[0], stop=kt == 1 and (a, c) == PARTS[-1])
                    last.then_inc(b_h, 1)

            def expert_of_block(n):
                return pe.value_load(bex[0:1, bass.ds(n, 1)], min_val=0, max_val=E - 1)

            fills.settled(B)
            pe.wait_ge(s_moew, 32)
            pe.wait_ge(s_setup, 14)
            pe.wait_ge(e_split, 2 * E)
            pe.wait_ge(r_blk, 1)
            block_transpose(0, 0)
            block_transpose(1, 1)
            hidden(0, 0, expert_of_block(0))
            with pe.Fori(0, NBLK // 2) as i:
                ex = [expert_of_block(2 * i)]
                for u in range(2):
                    n = 2 * i + u
                    for f in range(2):
                        pe.wait_ge(b_g, 2 * n + f + 1)
                        pe.wait_ge(b_tev, 2 * n + PRIMED)
                        for j in range(3):
                            last = pe.transpose(TT[f][:, j * P:(j + 1) * P], hs[:, (3 * f + j) * P:(3 * f + j + 1) * P], ident[:])
                        last.then_inc(b_t, 1)
                    ex.append(expert_of_block(n + 1))
                    block_transpose(n + 2, u)
                    hidden(n + 1, 1 - u, ex[u + 1])
                    pe.wait_ge(b_yev, n + PRIMED)
                    for j in range(FT):
                        if j % 3 == 0:
                            pe.wait_ge(b_tev, 2 * n + j // 3 + 1 + PRIMED)
                        last = pe.matmul(YB[u][:, 0:D], hT[:, j, :], wo2[:, bass.ds(ex[u] * FT + j, 1), :].rearrange("p o d -> p (o d)"),
                                         start=j == 0, stop=j == FT - 1)
                    last.then_inc(b_y, 1)

        @block.scalar
        def _(act):
            def tok_copy(k, out_, in_, bias=None):
                act.wait_ge(t_pe, k + 1)
                act.wait_ge(t_ev, k)
                if bias is None:
                    act.activation(out_, in_, ACT.Copy).then_inc(t_ev, 1)
                else:
                    act.activation(out_, in_, ACT.Identity, bias=bias).then_inc(t_ev, 1)

            for kt in range(2):
                for part in range(3):
                    if kt == part == 0:
                        act.wait_ge(s_attw, 16 * 6)
                    act.activation(wq[0][:, kt, part * DI:(part + 1) * DI], staged(kt, part), ACT.Copy).then_inc(w_high, 1)
            act.wait_ge(s_tokw, 16 * 11)
            k = 0
            for half in range(2):
                tok_copy(k, g1t[:, 4 * half:4 * half + 4, :].rearrange("p b t -> p (b t)"), bank[k % 4][0:96, :])
                k += 1
            for half in range(2):
                tok_copy(k, g2t[:, :, 64 * half:64 * half + 64].rearrange("p a (b t) -> p b a t", t=16),
                         bank[k % 4][0:96, :].rearrange("p (b a t) -> p b a t", a=8, t=16))
                k += 1
            tok_copy(k, e1[:], bank[k % 4][0:64, :])
            k += 1
            tok_copy(k, e2[:], bank[k % 4][:, 0:EMB])
            k += 1
            for j in range(4):
                tok_copy(k, ya[EMB:P, j * 512:(j + 1) * 512], bank[k % 4][EMB:P, :], bca[EMB:P, :])
                k += 1
            for j in range(4):
                tok_copy(k, yb[:, j * 512:(j + 1) * 512], bank[k % 4][0:EMB, :], bcb[:])
                k += 1
            for a in range(2):
                for half in range(2):
                    tok_copy(k, g0t[:, half * 512:(half + 1) * 512], bank[k % 4][0:48, :])
                    k += 1
                for half in range(2):
                    tok_copy(k, ya[0:EMB, :].rearrange("p (b a t) -> p b a t", a=2, t=P)[:, 4 * half:4 * half + 4, a, :],
                             bank[k % 4][0:EMB, :].rearrange("p (b t) -> p b t", t=P), bca[0:EMB, :])
                    k += 1
                k += B
            act.wait_ge(s_setup, 2)
            act.activation(unused[:], epsc[:], ACT.Sqrt)
            act.wait_ge(ln_var, 1)
            act.activation(rstd[:], mv[:, :, 1], ACT.Sqrt, bias=epsc[:]).then_inc(ln_std, 1)

            seen = FillCount(act)

            def full(j, b):
                act.wait_ge(x_full[j], seen.done(j, b) + 1)
                seen.n[j] += 1

            def tokens(b):
                for kt in range(2):
                    full(kt, b)
                    act.activation(xb[0][:, kt, :], bank[kt][0:KH, 0:SEQ], ACT.Copy).then_inc(x_hi[kt], 1)

            def values(b, m, j):
                if j == 0:
                    full(0, b)
                    act.activation(v[:, m, 0:384], bank[0][:, 0:384], ACT.Copy).then_inc(x_free[0], 1)
                else:
                    seen.n[1] += 1

            def projected(b, p, j):
                full(j, b)
                if j == 0:
                    act.activation(qT[p % 2][0][:], bank[0][:, 0:SEQ], ACT.Copy, scale=DH ** -0.5).then_inc(x_hi[0], 1)
                else:
                    act.activation(kz[p % 2][0][0][0:DH, :], bank[1][0:DH, 0:SEQ], ACT.Copy)
                    act.activation(kz[p % 2][1][0][DH:P, :], bank[1][DH:P, 0:SEQ], ACT.Copy).then_inc(x_hi[1], 1)

            def logits_copied(b):
                full(0, b)
                act.activation(logits[:].rearrange("p t e -> p (t e)"), bank[0][:, 0:MT * E], ACT.Copy).then_inc(x_free[0], 1)

            def ranks_copied(b):
                full(1, b)
                act.activation(rank[:].rearrange("p a n -> p (a n)"), bank[1][:, 0:2 * E * MT], ACT.Copy).then_inc(x_free[1], 1)

            def route_transposed(b, kt):
                full(kt, b)
                act.activation(xt[:, kt, :], bank[kt][0:KH, 0:SEQ], ACT.Copy).then_inc(x_free[kt], 1)

            def fill_copied(b, n, route, more):
                if n <= 7:
                    projected(b, n // 2 + 2, n % 2)
                elif not more:
                    pass
                elif n == 8:
                    tokens(b)
                elif n == 9:
                    projected(b, 0, 0)
                    projected(b, 0, 1)
                elif n == 10:
                    projected(b, 1, 0)
                if route:
                    if n == 5:
                        route_transposed(b, 0)
                    elif n == 6:
                        route_transposed(b, 1)
                    elif n == 7:
                        logits_copied(b)
                    elif n == 10:
                        ranks_copied(b)

            def exp(b, n, m):
                act.wait_ge(s_max, b * HEADS * MT + n * MT + m + 1)
                act.activation(pr[n % 2][:, m, :], bank[2 + m][:, 0:SEQ], ACT.Exp, bias=nmax[:, n % 2, m:m + 1],
                               accum_out=rsum[:, n % 2, m:m + 1]).then_inc(exp_done[m], 1)

            tokens(0)
            act.wait_ge(w_split, 6)
            for m in range(MT):
                for j in range(2):
                    values(0, m, j)
            projected(0, 0, 0)
            projected(0, 0, 1)
            projected(0, 1, 0)
            projected(0, 1, 1)
            for m in range(MT):
                exp(0, 0, m)

            def copy_rows(r):
                act.wait_ge(r_ln, r + 1)
                act.activation(rows[1][:, :, 0:D], rows[0][:, :, 0:D], ACT.Copy).then_inc(r_copy, 1)

            def gap_exp(r):
                act.wait_ge(r_gap, r + 1)
                act.activation(wts[:, 1, :], wts[:, 0, :], ACT.Exp).then_inc(r_exp, 1)

            def batch(b, route, more):
                for n in range(HEADS):
                    scored = more or n + 1 < HEADS
                    if scored:
                        act.wait_ge(p_free[(n + 1) % 2], b * (HEADS // 2) + (n + 1) // 2 + PRIMED)
                    for j in range(2):
                        e = n * MT + j
                        act.wait_ge(t_full, b * HEADS * MT + e + 1)
                        act.activation(pT[:, j, :], bank[5 + e % 2][:, 0:SEQ], ACT.Copy).then_inc(t_free[e % 2], 1)
                        if scored:
                            exp(b, n + 1, j)
                    if scored:
                        exp(b, n + 1, 2)
                    fill_copied(b, n, route, more)
                    if route and n == 4:
                        copy_rows(b - 1)
                    elif route and n == 9:
                        gap_exp(b - 1)
                if more:
                    for m in range(MT):
                        for j in range(2):
                            values(b, m, j)
                for m in range(MT):
                    seen.n[m % 2] += 1
                if more:
                    projected(b, 1, 1)

            batch(0, route=False, more=True)
            seen.enter_loop()
            with act.Fori(1, B - 1) as b:
                batch(b, route=True, more=True)
            seen.leave_loop()
            batch(B - 1, route=True, more=False)

            def up_weights_high(experts):
                for e in experts:
                    for kt in range(2):
                        w_ = (slice(0, KH + kt), kt, slice(e * F, (e + 1) * F))
                        act.activation(wih[w_], wi[w_], ACT.Copy).then_inc(e_high, 1)

            act.wait_ge(h_done, B * MT)
            act.wait_ge(s_upw, 32)
            up_weights_high(range(0, 5))
            for kt in range(2):
                route_transposed(B, kt)
            copy_rows(B - 1)
            logits_copied(B)
            gap_exp(B - 1)
            ranks_copied(B)
            up_weights_high(range(5, E))

            def block_high(u, it):
                act.wait_ge(b_x, 2 * it + u + 1)
                act.activation(xT[u][0][0:KH, :, :], bank[6][0:KH, 0:2 * P].rearrange("p (k n) -> p k n", k=2), ACT.Copy).then_inc(b_xhi, 1)

            for u in range(2):
                block_high(u, 0)
            for f in range(2):
                act.wait_ge(b_h, f + 1)
                act.activation(hs[:, f * FH:(f + 1) * FH], bank[f][:, 0:FH], ACT.Gelu).then_inc(b_g, 1)
            with act.Fori(0, NBLK // 2) as i:
                for u in range(2):
                    block_high(u, i + 1)
                    for f in range(2):
                        act.wait_ge(b_h, 4 * i + 2 * u + f + 3)
                        act.activation(hs[:, f * FH:(f + 1) * FH], bank[f][:, 0:FH], ACT.Gelu).then_inc(b_g, 1)
            for u in range(2):
                act.wait_ge(b_scat[u], 16 * (NBLK // 2))
            for b in range(B):
                act.dma_start(zc[1][b][:], routed_results(1, b)).then_inc(z_load[b], 16)

        @block.vector
        def _(dve):
            for kt in range(2):
                for part in range(3):
                    dve.wait_ge(w_high, kt * 3 + part + 1)
                    cols = slice(part * DI, (part + 1) * DI)
                    dve.tensor_tensor(wq[1][:, kt, cols], staged(kt, part), wq[0][:, kt, cols].bitcast(F32), ALU.subtract).then_inc(w_split, 1)
            dve.wait_ge(s_g1, 16 * G1)
            dve.tensor_copy(g1b[:].rearrange("p b (i c) -> p i b c", c=12),
                            g1[:].rearrange("p i (b c) -> p i b c", c=12)).then_inc(t_grp, 1)
            dve.wait_ge(s_g2, 16 * G2)
            dve.tensor_copy(g2b[:].rearrange("p b (i c) -> p i b c", c=48),
                            g2[:].rearrange("p i (b c) -> p i b c", c=48)).then_inc(t_grp, 1)

            def layer_stats(tiles):
                for t in tiles:
                    last = dve.bn_stats(stats[:, t, :], h[:, t, :])
                return last

            dve.wait_ge(s_txt, 16 * B)
            layer_stats([b * MT + 2 for b in range(B)])
            dve.wait_ge(s_tokw, 16 * 11)
            for a in range(2):
                dve.wait_ge(s_g0[a], 16 * GP)
                dve.tensor_copy(g0b[:, a].rearrange("p b (i c) -> p i b c", c=3),
                                g0[:, a].rearrange("p i (b c) -> p i b c", c=3)).then_inc(t_grp, 1)
                k = 14 + a * 12 + 4
                for b in range(B):
                    dve.wait_ge(t_pe, k + 1)
                    dve.tensor_tensor(h[:, b * MT + a, :], bank[k % 4][:, 0:D], bf_bc[:], ALU.add).then_inc(t_ev, 1)
                    k += 1
                    if b > 0:
                        dve.wait_ge(t_ev, k - 1)
                        last = layer_stats([(b - 1) * MT + a])
                    if a == 1 and b == B - 1:
                        last.then_inc(ln_chain, 1)
                        dve.wait_ge(ln_chain, 1)
                        for t in range(NT):
                            if t != (B - 1) * MT + 1:
                                dve.bn_aggr(mv[:, t, :], stats[:, t, :])
                dve.wait_ge(t_ev, k)
                if a == 1:
                    dve.engine_nop().then_inc(t_h, 16)
                last = layer_stats([(B - 1) * MT + a])
            last.then_inc(ln_chain, 1)
            dve.wait_ge(ln_chain, 2)
            t = (B - 1) * MT + 1
            dve.bn_aggr(mv[:, t, :], stats[:, t, :]).then_inc(ln_var, 1)
            dve.wait_ge(ln_std, 1)
            dve.reciprocal(rstd[:], rstd[:]).then_inc(ln_rstd, 1)
            dve.wait_ge(ln_rstd, 1)

            seen = FillCount(dve)
            highs = SplitCount(dve)

            def high(j, b):
                dve.wait_ge(x_hi[j], highs.done(j, b) + 1)
                highs.n[j] += 1
                seen.n[j] += 1

            def full(j, b):
                dve.wait_ge(x_full[j], seen.done(j, b) + 1)
                seen.n[j] += 1

            def normalised(nth):
                for m in range(MT):
                    t = nth * MT + m
                    last = dve.tensor_scalar(xnb[:, m, :], h_flat[:, bass.ds(t * D, D)], mv[:, bass.ds(t, 1), 0:1].rearrange("p o d -> p (o d)"),
                                             rstd[:, bass.ds(t, 1)], ALU.subtract, ALU.mult)
                last.then_inc(a_xn, 1)

            def tokens(b):
                for kt in range(2):
                    high(kt, b)
                    dve.tensor_tensor(xb[1][:, kt, :], bank[kt][0:KH, 0:SEQ], xb[0][:, kt, :].bitcast(F32), ALU.subtract).then_inc(x_free[kt], 1)

            def values(b, m, j):
                if j == 1:
                    full(1, b)
                    dve.tensor_copy(v[:, m, 384:768], bank[1][:, 0:384]).then_inc(x_free[1], 1)
                else:
                    seen.n[0] += 1

            def projected(b, p, j):
                high(j, b)
                if j == 0:
                    dve.scalar_tensor_tensor(out=qT[p % 2][1][:], in0=bank[0][:, 0:SEQ], scalar=DH ** -0.5, in1=qT[p % 2][0][:].bitcast(F32),
                                             op0=ALU.mult, op1=ALU.subtract).then_inc(x_free[0], 1)
                else:
                    for i, rows in ((0, slice(0, DH)), (1, slice(DH, P))):
                        last = dve.tensor_tensor(kz[p % 2][i][1][rows, :], bank[1][rows, 0:SEQ], kz[p % 2][i][0][rows, :].bitcast(F32), ALU.subtract)
                    last.then_inc(x_free[1], 1)

            steps = [0]
            STEPS = 7

            def step(instruction, r, last=False):
                steps[0] += 1
                instruction.then_inc(r_chain, 1)
                dve.wait_ge(r_chain, r * STEPS + steps[0])

            def route_norm(b, r):
                steps[0] = 0
                for j in range(2):
                    dve.wait_ge(x_free[j], seen.done(j, b) + PRIMED)
                for m in range(MT):
                    t = r * MT + m
                    last = dve.bn_stats(stats[:, m, :], h_flat[:, bass.ds(t * D, D)])
                step(last, r)
                dve.nop(nofuse=True)
                for m in range(MT):
                    last = dve.bn_aggr(mv2[:, m, :], stats[:, m, :])
                last.then_inc(r_var, 1)

            def route_rows(r):
                dve.wait_ge(r_free, r + PRIMED)
                dve.wait_ge(r_rstd, r + 1)
                for m in range(MT):
                    t = r * MT + m
                    last = dve.tensor_scalar(rows[0][:, m, 0:D], h_flat[:, bass.ds(t * D, D)], mv2[:, m, 0:1], rs[:, 1, m:m + 1],
                                             ALU.subtract, ALU.mult)
                last.then_inc(r_ln, 1)

            def route_choose(b, r):
                seen.n[0] += 1
                dve.wait_ge(x_free[0], seen.done(0, b) + PRIMED)
                dve.nop(nofuse=True)
                for m in range(MT):
                    last = dve.max(mx8[:, m, :], logits[:, m, :])
                step(last, r)
                dve.nop(nofuse=True)
                for m in range(MT):
                    last = dve.max_index(ix8[:, m, :], mx8[:, m, :], logits[:, m, :])
                step(last, r)

            def route_masks(r):
                dve.tensor_tensor(wts[:, 0, :], mx8[:, :, 1], mx8[:, :, 0], ALU.subtract).then_inc(r_gap, 1)
                for c in range(2):
                    last = dve.tensor_copy(ixf[:, c, :], ix8[:, :, c])
                step(last, r)
                for c in range(2):
                    last = dve.tensor_tensor(m01[:, c], eo[:], ixf[:, c:c + 1, :].broadcast_to([P, E, MT]), ALU.is_equal)
                step(last, r)
                dve.tensor_tensor(msum[:], m01[:, 0].rearrange("p e t -> p (e t)"), m01[:, 1].rearrange("p e t -> p (e t)"), ALU.add).then_inc(r_masks, 1)

            def route_weights(r):
                dve.wait_ge(r_exp, r + 1)
                step(dve.tensor_scalar(wts[:, 0, :], wts[:, 1, :], 1.0, None, ALU.add), r)
                step(dve.reciprocal(wts[:, 0, :], wts[:, 0, :]), r)
                dve.tensor_copy(rows[0][:, :, D + 1], wts[:, 0, :])
                dve.tensor_tensor(rows[1][:, :, D + 1], wts[:, 1, :], wts[:, 0, :], ALU.mult)
                for c in range(2):
                    dve.tensor_copy(rows[c][:, :, D].bitcast(I32), dest[:, c, bass.ds(r * MT, MT)])

            def route_ranks(b, r):
                seen.n[1] += 1
                dve.wait_ge(x_free[1], seen.done(1, b) + PRIMED)
                dve.nop(nofuse=True)
                dve.engine_nop().then_inc(r_ranks, 1)

            def fill_copied(b, n, more):
                if n <= 7:
                    projected(b, n // 2 + 2, n % 2)
                elif not more:
                    pass
                elif n == 8:
                    tokens(b)
                elif n == 9:
                    projected(b, 0, 0)
                    projected(b, 0, 1)
                elif n == 10:
                    projected(b, 1, 0)

            def route_step(b, n):
                r = b - 1
                if n == 0:
                    route_norm(b, r)
                elif n == 4:
                    route_rows(r)
                elif n == 5:
                    seen.n[0] += 1
                elif n == 6:
                    seen.n[1] += 1
                elif n == 8:
                    route_choose(b, r)
                elif n == 9:
                    route_masks(r)
                elif n == 10:
                    route_weights(r)
                elif n == 11:
                    route_ranks(b, r)

            def row_max(b, n, m):
                dve.wait_ge(s_full, b * HEADS * MT + n * MT + m + 1)
                dve.tensor_reduce(nmax[:, n % 2, m:m + 1], bank[2 + m][:, 0:SEQ], AX_X, ALU.max, negate=True).then_inc(s_max, 1)

            def pair_copied(b, p):
                dve.wait_ge(o_full, b * NPAIR + p + 1)
                dve.tensor_copy(oT[:, p, :], bank[7][:, 0:SEQ]).then_inc(o_free, 1)

            def normalise(b, n):
                for m in range(MT):
                    dve.wait_ge(exp_done[m], b * HEADS + n + 1 + PRIMED)
                dve.reciprocal(rinv[:, n % 2, :], rsum[:, n % 2, :]).then_inc(r_ready, 1)
                dve.wait_ge(r_ready, b * HEADS + n + 1)
                for m in range(MT):
                    last = dve.tensor_scalar(pr[n % 2][:, m, :], pr[n % 2][:, m, :], rinv[:, n % 2, m:m + 1], None, ALU.mult)
                last.then_inc(p_ready, 1)

            normalised(0)
            tokens(0)
            for m in range(MT):
                for j in range(2):
                    values(0, m, j)
            projected(0, 0, 0)
            projected(0, 0, 1)
            projected(0, 1, 0)
            projected(0, 1, 1)
            for m in range(MT):
                row_max(0, 0, m)
            normalise(0, 0)
            dve.wait_ge(s_rconst, 16 * 4)

            def batch(b, route, more):
                for n in range(HEADS):
                    p = n // 2
                    scored = more or n + 1 < HEADS
                    first, later = n in (8, 9, 10), n in (2, 4, 6)
                    if first:
                        fill_copied(b, n - 1, more)
                    if scored:
                        for m in range(MT):
                            row_max(b, n + 1, m)
                    if n % 2 == 0 and n > 0:
                        pair_copied(b, p - 1)
                    if n > 0 and not first and not later:
                        fill_copied(b, n - 1, more)
                    if route:
                        route_step(b, n)
                    e = n * MT + 2
                    dve.wait_ge(t_full, b * HEADS * MT + e + 1)
                    dve.tensor_copy(pT[:, 2, :], bank[5 + e % 2][:, 0:SEQ]).then_inc(t_free[e % 2], 1)
                    if later:
                        fill_copied(b, n - 1, more)
                    if scored:
                        normalise(b, n + 1)
                    if n == 6 and more:
                        normalised(b + 1)
                pair_copied(b, NPAIR - 1)
                if more:
                    for m in range(MT):
                        for j in range(2):
                            values(b, m, j)
                for m in range(MT):
                    full(m % 2, b)
                    t = b * MT + m
                    dst_ = h_flat[:, bass.ds(t * D, D)]
                    dve.tensor_tensor(dst_, dst_, bank[m % 2][:, 0:D], ALU.add).then_inc(x_free[m % 2], 1)
                if more:
                    projected(b, 1, 1)

            batch(0, route=False, more=True)
            seen.enter_loop()
            highs.enter_loop()
            with dve.Fori(1, B - 1) as b:
                batch(b, route=True, more=True)
                assert tuple(seen.n) == seen.per_batch and tuple(highs.n) == highs.per_batch
                assert steps[0] == STEPS
            seen.leave_loop()
            highs.leave_loop()
            batch(B - 1, route=True, more=False)
            for j in range(2):
                dve.wait_ge(x_free[j], seen.n[j] + PRIMED)
            dve.engine_nop().then_inc(h_done, B * MT)

            def up_weights_low(chunks):
                for i in chunks:
                    e, kt = i // 2, i % 2
                    dve.wait_ge(e_high, i + 1)
                    w_ = (slice(0, KH + kt), kt, slice(e * F, (e + 1) * F))
                    dve.tensor_tensor(wi[w_].bitcast(F32R), wi[w_], wih[w_].bitcast(F32), ALU.subtract).then_inc(e_split, 1)

            r = B - 1
            route_norm(B, r)
            up_weights_low(range(0, 5))
            route_rows(r)
            up_weights_low(range(5, 10))
            seen.n = [seen.n[j] + 1 for j in range(2)]
            route_choose(B, r)
            route_masks(r)
            route_weights(r)
            route_ranks(B, r)
            up_weights_low(range(10, 14))
            dve.wait_ge(r_slot, B)
            step(dve.tensor_copy(ends[:], nxt[0:1, :]), r)
            dve.engine_nop().then_inc(r_end, 1)
            step(dve.tensor_scalar(base[:], eo[:, :, 0], -float(REGION), float(P - 1), ALU.mult, ALU.add), r)
            step(dve.tensor_tensor(nbi[:], nxt[:], base[:], ALU.add), r)
            step(dve.tensor_scalar(nbi[:], nbi[:], 7, None, ALU.logical_shift_right), r)
            step(dve.tensor_copy(nbf[:], nbi[:]), r)
            step(dve.tensor_tensor_scan(binc[:], ones[:, 0:E], nbf[:], 0.0, ALU.mult, ALU.add), r)
            step(dve.tensor_tensor(bcmp[:], binc[0:1, :].rearrange("p (o e) -> p o e", o=1).broadcast_to([1, NBLK_LOADED, E]), bn[:], ALU.is_le), r)
            step(dve.tensor_reduce(bexf[:], bcmp[:], AX_X, ALU.add), r)
            step(dve.tensor_scalar(bexf[:], bexf[:], float(E - 1), None, ALU.min), r)
            step(dve.tensor_copy(bex[:], bexf[:]), r)
            step(dve.tensor_scalar(nbf[:], nbf[:], -float(P), float(REGION), ALU.mult, ALU.add), r)
            step(dve.tensor_tensor(bcmp[:], bcmp[:], nbf[0:1, :].rearrange("p (o e) -> p o e", o=1).broadcast_to([1, NBLK_LOADED, E]), ALU.mult), r)
            step(dve.tensor_reduce(bexf[:], bcmp[:], AX_X, ALU.add), r)
            step(dve.tensor_scalar(bn[:, :, 0], bn[:, :, 0], float(P), None, ALU.mult), r)
            step(dve.tensor_tensor(bexf[:], bexf[:], bn[:, :, 0], ALU.add), r)
            step(dve.tensor_copy(brow[:], bexf[:]), r)
            dve.engine_nop().then_inc(r_blk, 1)
            up_weights_low(range(14, 2 * E))

            def block_copy(u, it):
                dve.wait_ge(b_xhi, 2 * it + u + 1)
                dve.tensor_tensor(xT[u][1][0:KH, :, :], bank[6][0:KH, 0:2 * P].rearrange("p (k n) -> p k n", k=2),
                                  xT[u][0][0:KH, :, :].bitcast(F32), ALU.subtract).then_inc(b_xev, 1)

            def address_copy(u, it):
                dve.wait_ge(b_load[u], 16 * (it + 1))
                dve.tensor_copy(dst_next[u][:].bitcast(I32), xr[u][:, D:ROW].bitcast(I32)).then_inc(b_addr, 1)

            dve.wait_ge(s_moew, 32)
            for u in range(2):
                block_copy(u, 0)
                address_copy(u, 0)
            with dve.Fori(0, NBLK // 2) as i:
                for u in range(2):
                    for f in range(2):
                        dve.wait_ge(b_t, 4 * i + 2 * u + f + 1)
                        dve.tensor_copy(hT[:, 3 * f:3 * f + 3, :].rearrange("p a b -> p (a b)"), bank[2 + f][:, 0:FH]).then_inc(b_tev, 1)
                    block_copy(u, i + 1)
                    expert = dve.value_load(bex[0:1, bass.ds(2 * i + u, 1)], min_val=0, max_val=E - 1)
                    dve.wait_ge(y_free[u], i + PRIMED)
                    dve.wait_ge(b_addr, 2 * i + u + 1)
                    dve.tensor_copy(dst[u][:].bitcast(I32), dst_next[u][:].bitcast(I32)).then_inc(b_dst, 1)
                    dve.wait_ge(b_y, 2 * i + u + 1)
                    dve.tensor_tensor(yv[u][:], bank[4 + u][:, 0:D], bo_bc[:, bass.ds(expert * D, D)], ALU.add).then_inc(b_yev, 1)
                    dve.wait_ge(b_yev, 2 * i + u + 1 + PRIMED)
                    dve.wait_ge(b_dst, 2 * i + u + 1)
                    dve.tensor_scalar(yv[u][:], yv[u][:], dst[u][:, 1:2], None, ALU.mult).then_inc(b_yw, 1)
                    address_copy(u, i + 1)

            for b in range(B):
                dve.wait_ge(z_load[b], 32)
                hb = h[:, b * MT:(b + 1) * MT, :]
                dve.tensor_tensor(hb, hb, zc[0][b][:], ALU.add).then_inc(z_chain, 1)
                dve.wait_ge(z_chain, b + 1)
                dve.tensor_tensor(hb, hb, zc[1][b][:], ALU.add).then_inc(z_sum, 1)


def interpolation(n_in, n_out):
    pos = (np.arange(n_out, dtype=np.float32) + np.float32(0.5)) * np.float32(n_in / n_out) - np.float32(0.5)
    pos = np.clip(pos, 0.0, n_in - 1).astype(np.float32)
    lo = np.floor(pos).astype(np.int64)
    hi = np.minimum(lo + 1, n_in - 1)
    w = (pos - lo).astype(np.float32)
    m = np.zeros((n_in, n_out), np.float32)
    m[lo, np.arange(n_out)] += np.float32(1.0) - w
    m[hi, np.arange(n_out)] += w
    return m


def shape_constants():
    a1 = interpolation(64, TOK_IMG)
    a2 = interpolation(16, TOK_IMG)
    big = np.zeros((P, B, TOK_IMG), np.float32)
    for b in range(B):
        big[16 * b:16 * b + 16, b] = a2
    p = np.arange(P)
    dest = np.stack([c * NTOK + np.arange(NT)[None, :] * P + p[:, None] for c in range(2)], 1).astype(np.int32)
    pads = np.zeros((P, E, ROW), np.float32)
    pads[:, :, D] = (2 * NTOK + np.arange(E)[None, :] * P + p[:, None]).astype(np.int32).view(np.float32)
    spare = np.zeros((SPARE * P, ROW), np.float32)
    spare[:, D] = (2 * NTOK + E * P + np.arange(SPARE * P)).astype(np.int32).view(np.float32)
    return {
        "ident_c": np.eye(P, dtype=np.float32),
        "tri_c": np.triu(np.ones((P, P), np.float32), 1),
        "A1": a1, "A2": big,
        "expert_of": np.broadcast_to(np.arange(E, dtype=np.float32)[None, :, None], (P, E, MT)).copy(),
        "block_no": np.broadcast_to(np.arange(NBLK_LOADED, dtype=np.float32)[None, :, None], (1, NBLK_LOADED, E)).copy(),
        "dest_c": dest,
        "region_c": np.broadcast_to(REGION * np.arange(E, dtype=np.float32)[None, :], (P, E)).copy(),
        "pad_rows": pads,
        "spare_rows": spare,
    }


def kernel(x, txt, L0_tok_W0, L0_tok_b0, L0_tok_W1, L0_tok_b1, L0_tok_W2, L0_tok_b2, L0_tok_Wf, L0_tok_bf,
           L0_tok_idx0, L0_tok_idx1, L0_tok_idx2, L0_attn_w_qkv, L0_attn_w_o, L0_ffn_Wr, L0_ffn_Wi, L0_ffn_bi,
           L0_ffn_Wo, L0_ffn_bo):
    import concourse.bacc as bacc
    from concourse.bass_utils import run_bass_kernel_spmd

    x = np.asarray(x)

    def patches(p):
        n = IMG // p
        return x.reshape(B, CH, n, p, n, p).transpose(2, 4, 0, 3, 5, 1)

    def halves(w):
        return w.reshape(2, KH, -1).transpose(1, 0, 2)

    a = np.asarray
    arrays = {
        "xp0": patches(1).reshape(4096, B * 3),
        "xp1": patches(2).reshape(1024, B * 12),
        "xp2": patches(4).reshape(256, B * 48),
        "txt": a(txt),
        "W0T": a(L0_tok_W0).T, "b0": a(L0_tok_b0).reshape(-1, 1),
        "W1T": a(L0_tok_W1).T.reshape(2, 96, EMB).transpose(1, 0, 2), "b1": a(L0_tok_b1).reshape(-1, 1),
        "W2T": a(L0_tok_W2).T.reshape(8, 96, EMB).transpose(1, 0, 2), "b2": a(L0_tok_b2).reshape(-1, 1),
        "WfT": a(L0_tok_Wf).T, "bf": a(L0_tok_bf).reshape(1, -1),
        "idx0": a(L0_tok_idx0), "idx1": a(L0_tok_idx1), "idx2": a(L0_tok_idx2),
        "wqkv": halves(a(L0_attn_w_qkv).transpose(2, 1, 0, 3).reshape(D, 3 * DI)),
        "wo": a(L0_attn_w_o).reshape(NPAIR, P, D).transpose(1, 0, 2),
        "WrT": halves(a(L0_ffn_Wr).T),
        "WiT": halves(a(L0_ffn_Wi).transpose(2, 0, 1).reshape(D, E * F)),
        "bi": a(L0_ffn_bi).reshape(1, -1),
        "WoT": a(L0_ffn_Wo).transpose(0, 2, 1).reshape(E * FT, P, D).transpose(1, 0, 2),
        "bo": a(L0_ffn_bo).reshape(1, -1),
    }
    arrays.update(shape_constants())
    nc = bacc.Bacc("TRN2", target_bir_lowering=False, num_devices=1)
    given, aps = {}, {}
    for name, value in arrays.items():
        value = np.ascontiguousarray(value)
        given["in_" + name] = value
        aps[name] = nc.dram_tensor("in_" + name, value.shape, mybir.dt.from_np(value.dtype), kind="ExternalInput").ap()
    aps["xg"] = nc.dram_tensor("routed_rows", (SLOTS, ROW), F32, kind="Internal").ap()
    aps["z"] = nc.dram_tensor("routed_results", (2 * NTOK + (E + SPARE) * P, D), F32, kind="Internal").ap()
    aps["out"] = nc.dram_tensor("out_0", (B, SEQ, D), F32, kind="ExternalOutput").ap()
    fused_layer_kernel(nc, **aps)
    result = run_bass_kernel_spmd(nc, [given], core_ids=[0])
    return result.results[0]["out_0"]
```
